# Optimizing a Trainium2 kernel written in Bass

```python
import numpy as np
import jax
import jax.numpy as jnp

def _softmax(x, axis=-1):
    return jax.nn.softmax(x, axis=axis)

def _gelu(x):
    return jax.nn.gelu(x, approximate=True)

def _silu(x):
    return jax.nn.silu(x)

def _sigmoid(x):
    return jax.nn.sigmoid(x)

def _layernorm(x, axis=-1, eps=1e-05):
    m = jnp.mean(x, axis=axis, keepdims=True)
    v = jnp.var(x, axis=axis, keepdims=True)
    return (x - m) / jnp.sqrt(v + eps)

def _scatter_add(tgt, idx, src, axis=0):
    return tgt.at[idx].add(src)

def _segment_sum(src, seg, n):
    return jax.ops.segment_sum(src, seg, n)
kernel_name = 'mk_adj_resnorm_d4_adj_r2_c7b944'

def setup_inputs(seed: int=0):
    np.random.seed(seed)
    _w = jnp.asarray

    def _rec_inputs():
        import jax
        import jax.numpy as jnp
        _gk = jax.random.key(seed)
        x = -0.0005207 + 1.001 * jax.random.normal(jax.random.fold_in(_gk, 1), (4096, 128), jnp.float32)
        _a = jax.random.bernoulli(jax.random.fold_in(_gk, 2), 0.000488281, (4096, 4096))
        _a = jnp.logical_or(_a, jnp.swapaxes(_a, -1, -2))
        _a = jnp.logical_or(_a, jnp.eye(4096, dtype=bool))
        _af = _a.astype(jnp.float32)
        _af = _af * jax.random.uniform(jax.random.fold_in(_gk, 3), (4096, 4096), jnp.float32, 0.05, 1)
        adj = _af
        return (x, adj)
    x, adj = _rec_inputs()

    def _L0_gnn_setup():
        import jax, jax.numpy as jnp
        import numpy as np
        N, DIM = (8192, 128)

        def _gru_cell(x, h, W_ih, W_hh, b_ih, b_hh):
            gi = x @ W_ih.T + b_ih
            gh = h @ W_hh.T + b_hh
            i_r, i_z, i_n = jnp.split(gi, 3, axis=-1)
            h_r, h_z, h_n = jnp.split(gh, 3, axis=-1)
            r = jax.nn.sigmoid(i_r + h_r)
            z = jax.nn.sigmoid(i_z + h_z)
            n = jnp.tanh(i_n + r * h_n)
            return (1.0 - z) * n + z * h
        key = jax.random.key(seed)
        ks = jax.random.split(key, 8)
        states = jax.random.normal(ks[0], (N, DIM), dtype=jnp.float32)
        adj = jax.random.uniform(ks[1], (N, N), dtype=jnp.float32)
        s = 1.0 / np.sqrt(DIM)
        W_msg = jax.random.uniform(ks[2], (DIM, DIM), minval=-s, maxval=s, dtype=jnp.float32)
        b_msg = jax.random.uniform(ks[3], (DIM,), minval=-s, maxval=s, dtype=jnp.float32)
        W_ih = jax.random.uniform(ks[4], (3 * DIM, DIM), minval=-s, maxval=s, dtype=jnp.float32)
        W_hh = jax.random.uniform(ks[5], (3 * DIM, DIM), minval=-s, maxval=s, dtype=jnp.float32)
        b_ih = jax.random.uniform(ks[6], (3 * DIM,), minval=-s, maxval=s, dtype=jnp.float32)
        b_hh = jax.random.uniform(ks[7], (3 * DIM,), minval=-s, maxval=s, dtype=jnp.float32)
        return {'states': states, 'adj': adj, 'W_msg': W_msg, 'b_msg': b_msg, 'W_ih': W_ih, 'W_hh': W_hh, 'b_ih': b_ih, 'b_hh': b_hh}
    _L0_gnn_all = _L0_gnn_setup()
    _L0_gnn_in = {k: v for k, v in _L0_gnn_all.items() if k in ('W_msg', 'b_msg', 'W_ih', 'W_hh', 'b_ih', 'b_hh')}
    del _L0_gnn_all

    def _L1_gnn_setup():
        import jax, jax.numpy as jnp
        import numpy as np
        EPS = 1e-07
        MAX_TANH = 1.0 - 1e-06

        def _norm(v):
            return jnp.maximum(jnp.linalg.norm(v, axis=-1, keepdims=True), EPS)

        def log_map_zero(y):
            n = _norm(y)
            return jnp.arctanh(jnp.clip(n, 0.0, MAX_TANH)) * y / n

        def exp_map_zero(v):
            n = _norm(v)
            return jnp.tanh(n) * v / n

        def h_add(x, y):
            xy = jnp.sum(x * y, axis=-1, keepdims=True)
            x2 = jnp.sum(x * x, axis=-1, keepdims=True)
            y2 = jnp.sum(y * y, axis=-1, keepdims=True)
            num = (1.0 + 2.0 * xy + y2) * x + (1.0 - x2) * y
            den = 1.0 + 2.0 * xy + x2 * y2
            return num / jnp.maximum(den, EPS)

        def h_mul(x, W):
            return exp_map_zero(log_map_zero(x) @ W)
        key = jax.random.key(seed)
        k1, k2, k3, k4 = jax.random.split(key, 4)
        N, F_IN, F_OUT = (4096, 128, 128)
        x = 0.05 * jax.random.normal(k1, (N, F_IN), dtype=jnp.float32)
        a = (jax.random.uniform(k2, (N, N)) < 0.01).astype(jnp.float32)
        adj = a / jnp.maximum(a.sum(axis=1, keepdims=True), 1.0)
        lim_e = np.sqrt(6.0 / (F_IN + F_IN)) * np.sqrt(2.0)
        lim_l = np.sqrt(6.0 / (2 * F_IN + F_OUT)) * np.sqrt(2.0)
        embed = jax.random.uniform(k3, (F_IN, F_IN), minval=-lim_e, maxval=lim_e, dtype=jnp.float32)
        layer = jax.random.uniform(k4, (2 * F_IN, F_OUT), minval=-lim_l, maxval=lim_l, dtype=jnp.float32)
        embed_bias = jnp.zeros((F_IN,), dtype=jnp.float32)
        layer_bias = jnp.zeros((F_OUT,), dtype=jnp.float32)
        return {'x': x, 'adj': adj, 'embed': embed, 'layer': layer, 'embed_bias': embed_bias, 'layer_bias': layer_bias}
    _L1_gnn_all = _L1_gnn_setup()
    _L1_gnn_in = {k: v for k, v in _L1_gnn_all.items() if k in ('embed', 'layer', 'embed_bias', 'layer_bias')}
    del _L1_gnn_all

    def _L2_gnn_setup():
        import jax, jax.numpy as jnp
        import numpy as np
        N = 4096
        D = 128
        DENSITY = 0.01
        NEG_INF = -1000000000.0
        key = jax.random.key(seed)
        k_emb, k_mask, k_vals, k_h = jax.random.split(key, 4)
        emb = jax.random.normal(k_emb, (N, D), dtype=jnp.float32)
        u = jax.random.uniform(k_mask, (N, N), dtype=jnp.float32)
        vals = jax.random.uniform(k_vals, (N, N), dtype=jnp.float32)
        adj = jnp.where(u < DENSITY, vals, 0.0)
        idx = jnp.arange(N)
        adj = adj.at[idx, idx].set(1.0)
        H_v = 0.1 * jax.random.normal(k_h, (D, 1), dtype=jnp.float32)
        return {'emb': emb, 'adj': adj, 'H_v': H_v}
    _L2_gnn_all = _L2_gnn_setup()
    _L2_gnn_in = {k: v for k, v in _L2_gnn_all.items() if k in ('H_v',)}
    del _L2_gnn_all

    def _L3_gnn_setup():
        import jax, jax.numpy as jnp
        import numpy as np
        NEG_SLOPE = 0.01
        N_U, N_V = (4096, 4096)
        U_F, V_F = (128, 128)
        HIDS = [128, 128]
        NUM_ROUNDS = 3

        def _glorot(key, fan_in, fan_out):
            lim = np.sqrt(6.0 / (fan_in + fan_out)).astype(np.float32)
            return jax.random.uniform(key, (fan_in, fan_out), jnp.float32, -lim, lim)

        def _mlp(x, W1, b1, W2, b2, W3, b3):
            a = jax.nn.leaky_relu
            x = a(x @ W1 + b1, NEG_SLOPE)
            x = a(x @ W2 + b2, NEG_SLOPE)
            return a(x @ W3 + b3, NEG_SLOPE)
        key = jax.random.key(seed)
        ks = jax.random.split(key, 12)
        inp = {'u_node_feats': jax.random.normal(ks[0], (N_U, U_F), jnp.float32), 'v_node_feats': jax.random.normal(ks[1], (N_V, V_F), jnp.float32), 'uv_adj_mat': jax.random.uniform(ks[2], (N_V, N_U), jnp.float32), 'vu_adj_mat': jax.random.uniform(ks[3], (N_U, N_V), jnp.float32)}
        dims_uv = [U_F] + HIDS + [V_F]
        dims_vu = [V_F] + HIDS + [U_F]
        k = 4
        for tag, dims in (('uv', dims_uv), ('vu', dims_vu)):
            for i in range(3):
                inp[f'{tag}_W{i + 1}'] = _glorot(ks[k], dims[i], dims[i + 1])
                k += 1
                inp[f'{tag}_b{i + 1}'] = jnp.zeros((dims[i + 1],), jnp.float32)
        return inp
    _L3_gnn_all = _L3_gnn_setup()
    _L3_gnn_in = {k: v for k, v in _L3_gnn_all.items() if k in ('v_node_feats', 'uv_W1', 'uv_b1', 'uv_W2', 'uv_b2', 'uv_W3', 'uv_b3', 'vu_W1', 'vu_b1', 'vu_W2', 'vu_b2', 'vu_W3', 'vu_b3')}
    del _L3_gnn_all
    return {'x': x, 'adj': adj, 'L0_gnn_W_msg': _L0_gnn_in['W_msg'], 'L0_gnn_b_msg': _L0_gnn_in['b_msg'], 'L0_gnn_W_ih': _L0_gnn_in['W_ih'], 'L0_gnn_W_hh': _L0_gnn_in['W_hh'], 'L0_gnn_b_ih': _L0_gnn_in['b_ih'], 'L0_gnn_b_hh': _L0_gnn_in['b_hh'], 'L1_gnn_embed': _L1_gnn_in['embed'], 'L1_gnn_layer': _L1_gnn_in['layer'], 'L1_gnn_embed_bias': _L1_gnn_in['embed_bias'], 'L1_gnn_layer_bias': _L1_gnn_in['layer_bias'], 'L2_gnn_H_v': _L2_gnn_in['H_v'], 'L3_gnn_v_node_feats': _L3_gnn_in['v_node_feats'], 'L3_gnn_uv_W1': _L3_gnn_in['uv_W1'], 'L3_gnn_uv_b1': _L3_gnn_in['uv_b1'], 'L3_gnn_uv_W2': _L3_gnn_in['uv_W2'], 'L3_gnn_uv_b2': _L3_gnn_in['uv_b2'], 'L3_gnn_uv_W3': _L3_gnn_in['uv_W3'], 'L3_gnn_uv_b3': _L3_gnn_in['uv_b3'], 'L3_gnn_vu_W1': _L3_gnn_in['vu_W1'], 'L3_gnn_vu_b1': _L3_gnn_in['vu_b1'], 'L3_gnn_vu_W2': _L3_gnn_in['vu_W2'], 'L3_gnn_vu_b2': _L3_gnn_in['vu_b2'], 'L3_gnn_vu_W3': _L3_gnn_in['vu_W3'], 'L3_gnn_vu_b3': _L3_gnn_in['vu_b3']}

def reference(x, adj, L0_gnn_W_msg, L0_gnn_b_msg, L0_gnn_W_ih, L0_gnn_W_hh, L0_gnn_b_ih, L0_gnn_b_hh, L1_gnn_embed, L1_gnn_layer, L1_gnn_embed_bias, L1_gnn_layer_bias, L2_gnn_H_v, L3_gnn_v_node_feats, L3_gnn_uv_W1, L3_gnn_uv_b1, L3_gnn_uv_W2, L3_gnn_uv_b2, L3_gnn_uv_W3, L3_gnn_uv_b3, L3_gnn_vu_W1, L3_gnn_vu_b1, L3_gnn_vu_W2, L3_gnn_vu_b2, L3_gnn_vu_W3, L3_gnn_vu_b3):
    import jax
    import jax.numpy as jnp

    def _L0_gnn_ref(states, adj, W_msg, b_msg, W_ih, W_hh, b_ih, b_hh):
        import jax, jax.numpy as jnp
        import numpy as np
        N, DIM = (8192, 128)

        def _gru_cell(x, h, W_ih, W_hh, b_ih, b_hh):
            gi = x @ W_ih.T + b_ih
            gh = h @ W_hh.T + b_hh
            i_r, i_z, i_n = jnp.split(gi, 3, axis=-1)
            h_r, h_z, h_n = jnp.split(gh, 3, axis=-1)
            r = jax.nn.sigmoid(i_r + h_r)
            z = jax.nn.sigmoid(i_z + h_z)
            n = jnp.tanh(i_n + r * h_n)
            return (1.0 - z) * n + z * h
        agg = adj @ states
        msg = jax.nn.relu(agg @ W_msg.T + b_msg)
        return _gru_cell(msg, states, W_ih, W_hh, b_ih, b_hh)

    def _L1_gnn_ref(x, adj, embed, layer, embed_bias, layer_bias):
        import jax, jax.numpy as jnp
        import numpy as np
        EPS = 1e-07
        MAX_TANH = 1.0 - 1e-06

        def _norm(v):
            return jnp.maximum(jnp.linalg.norm(v, axis=-1, keepdims=True), EPS)

        def log_map_zero(y):
            n = _norm(y)
            return jnp.arctanh(jnp.clip(n, 0.0, MAX_TANH)) * y / n

        def exp_map_zero(v):
            n = _norm(v)
            return jnp.tanh(n) * v / n

        def h_add(x, y):
            xy = jnp.sum(x * y, axis=-1, keepdims=True)
            x2 = jnp.sum(x * x, axis=-1, keepdims=True)
            y2 = jnp.sum(y * y, axis=-1, keepdims=True)
            num = (1.0 + 2.0 * xy + y2) * x + (1.0 - x2) * y
            den = 1.0 + 2.0 * xy + x2 * y2
            return num / jnp.maximum(den, EPS)

        def h_mul(x, W):
            return exp_map_zero(log_map_zero(x) @ W)
        h = h_mul(x, embed)
        h = h_add(h, embed_bias[None, :])
        neigh = exp_map_zero(adj @ log_map_zero(h))
        out = h_mul(jnp.concatenate((x, neigh), axis=1), layer)
        out = h_add(out, layer_bias[None, :])
        return out

    def _L2_gnn_ref(emb, adj, H_v):
        import jax, jax.numpy as jnp
        import numpy as np
        N = 4096
        D = 128
        DENSITY = 0.01
        NEG_INF = -1000000000.0
        s = (emb @ H_v)[:, 0]
        mask = adj != 0.0
        logits = jnp.where(mask, adj * s[None, :], NEG_INF)
        alpha = jax.nn.softmax(logits, axis=1)
        alpha = jnp.where(mask, alpha, 0.0)
        return alpha @ emb

    def _L3_gnn_ref(u_node_feats, v_node_feats, uv_adj_mat, vu_adj_mat, uv_W1, uv_b1, uv_W2, uv_b2, uv_W3, uv_b3, vu_W1, vu_b1, vu_W2, vu_b2, vu_W3, vu_b3):
        import jax, jax.numpy as jnp
        import numpy as np
        NEG_SLOPE = 0.01
        N_U, N_V = (4096, 4096)
        U_F, V_F = (128, 128)
        HIDS = [128, 128]
        NUM_ROUNDS = 3

        def _glorot(key, fan_in, fan_out):
            lim = np.sqrt(6.0 / (fan_in + fan_out)).astype(np.float32)
            return jax.random.uniform(key, (fan_in, fan_out), jnp.float32, -lim, lim)

        def _mlp(x, W1, b1, W2, b2, W3, b3):
            a = jax.nn.leaky_relu
            x = a(x @ W1 + b1, NEG_SLOPE)
            x = a(x @ W2 + b2, NEG_SLOPE)
            return a(x @ W3 + b3, NEG_SLOPE)
        u, v = (u_node_feats, v_node_feats)
        for _ in range(NUM_ROUNDS):
            v = _mlp(uv_adj_mat @ u, uv_W1, uv_b1, uv_W2, uv_b2, uv_W3, uv_b3)
            u = _mlp(vu_adj_mat @ v, vu_W1, vu_b1, vu_W2, vu_b2, vu_W3, vu_b3)
        return v
    x = _layernorm(x + _L0_gnn_ref(x, adj, L0_gnn_W_msg, L0_gnn_b_msg, L0_gnn_W_ih, L0_gnn_W_hh, L0_gnn_b_ih, L0_gnn_b_hh), axis=-1)
    x = _layernorm(x + _L1_gnn_ref(x, adj, L1_gnn_embed, L1_gnn_layer, L1_gnn_embed_bias, L1_gnn_layer_bias), axis=-1)
    x = _layernorm(x + _L2_gnn_ref(x, adj, L2_gnn_H_v), axis=-1)
    x = _layernorm(x + _L3_gnn_ref(x, L3_gnn_v_node_feats, adj, adj, L3_gnn_uv_W1, L3_gnn_uv_b1, L3_gnn_uv_W2, L3_gnn_uv_b2, L3_gnn_uv_W3, L3_gnn_uv_b3, L3_gnn_vu_W1, L3_gnn_vu_b1, L3_gnn_vu_W2, L3_gnn_vu_b2, L3_gnn_vu_W3, L3_gnn_vu_b3), axis=-1)
    return x

_drawn_inputs = setup_inputs


def setup_inputs(seed=0):
    import zlib

    import numpy as np

    out = dict(_drawn_inputs(seed))
    spreads = {'L1_gnn_embed_bias': (0.0, 0.8),
     'L1_gnn_layer_bias': (0.0, 0.8),
     'L3_gnn_uv_b1': (0.0, 0.1),
     'L3_gnn_uv_b2': (0.0, 0.1),
     'L3_gnn_uv_b3': (0.0, 0.1),
     'L3_gnn_vu_b1': (0.0, 0.1),
     'L3_gnn_vu_b2': (0.0, 0.1),
     'L3_gnn_vu_b3': (0.0, 0.1)}
    factors = {'L0_gnn_b_msg': 7.45, 'L0_gnn_b_hh': 4.601, 'L1_gnn_embed': 7.213}
    for name, (base, spread) in spreads.items():
        noise = np.random.default_rng([zlib.crc32(name.encode()), seed]).standard_normal(out[name].shape)
        drawn = base * np.exp(spread * noise) if base else spread * noise
        out[name] = jnp.asarray(drawn.astype(out[name].dtype))
    for name, factor in factors.items():
        out[name] = (out[name] * factor).astype(out[name].dtype)
    return out
```

```python
import concourse.bass as bass
from concourse import mybir
from contextlib import ExitStack

FP32 = mybir.dt.float32
ALU = mybir.AluOpType
ACT = mybir.ActivationFunctionType
AX = mybir.AxisListType

N, F = 4096, 128
P = 128
TILES = N // P
BW = 512
BLOCKS = N // BW
QT = BW // P
CHUNKS = TILES // QT
NEG = -1e9
EPS = 1e-7
MAX_TANH = 1.0 - 1e-6
LN_EPS = 1e-5
SLOPE = 0.01

GRU, HYPER, ATTN, MLP0, ROUNDS = 0, 1, 2, 3, 5
PASSES = MLP0 + ROUNDS
SMALL = {GRU: 6, HYPER: 6, ATTN: 1}

(W_MSG, W_IH, W_HH, W_EMBED, W_TOP, W_BOT, W_UV, W_VU, W_ALL) = (0, 1, 4, 7, 8, 9, 10, 13, 16)
(C_MSG, C_IH, C_HH, C_UV, C_VU, C_ALL) = (0, 1, 4, 7, 9, 11)
R_EMBED, R_LAYER, R_HV, R_UV, R_VU, R_ALL = range(6)


class Steps:

    def __init__(self, engine, sem):
        self.engine, self.sem, self.n = engine, sem, 0

    def then(self, instruction):
        self.n += 1
        instruction.then_inc(self.sem, 1)
        self.engine.wait_ge(self.sem, self.n)

    def restart(self):
        self.engine.sem_clear(self.sem)
        self.n = 0


def small_before(layer, b):
    at = {GRU: 0, HYPER: SMALL[GRU] * BLOCKS, ATTN: (SMALL[GRU] + SMALL[HYPER]) * BLOCKS,
          PASSES - 1: (SMALL[GRU] + SMALL[HYPER] + SMALL[ATTN]) * BLOCKS}[layer]
    return b * SMALL.get(layer, 1) + at


def build(nc, adj, x_nodes, x_feats, weights, columns, rows, out):
    with ExitStack() as ctx:
        def sb(name, *shape):
            return ctx.enter_context(nc.sbuf_tensor(name, [P, *shape], FP32))

        def sem(name):
            return ctx.enter_context(nc.semaphore(name))

        ring = sb("ring", CHUNKS, QT, BW)
        nodes = [sb(f"nodes{i}", TILES, F) for i in range(4)]
        x_in, x_gru, lifted, top_part = nodes
        x_hyper, x_attn = x_gru, lifted
        rounds = [x_attn, x_in, x_gru, x_in, x_gru]
        written = [x_in, x_gru, x_in, x_gru, None]
        xT = sb("xT", N)
        w = sb("w", W_ALL, P)
        cols = sb("cols", C_ALL)
        bias_rz = sb("bias_rz", 2)
        brow = sb("brow", R_ALL, F)
        ident = sb("ident", P)
        ones = sb("ones", P)
        score = sb("score", TILES)
        x_sq = sb("x_sq", TILES)
        bias_sq = sb("bias_sq", 2)
        aggT = sb("aggT", BW)
        sqT = sb("sqT", BW)
        t = [sb(f"t{i}", BW) for i in range(6)]
        big = sb("big", QT, BW)
        valid = sb("valid", 2, BW)
        mx = sb("mx", QT, BW)
        stats = sb("stats", QT, 6)
        mv = sb("mv", QT, 2)
        s_in = sb("s_in", 2 * QT)
        s_out = sb("s_out", 2 * QT)
        sc = sb("sc", 24, QT)

        acc = ctx.enter_context(nc.psum_tensor("acc", [P, 2, BW], FP32))
        epi = ctx.enter_context(nc.psum_tensor("epi", [P, 6, BW], FP32))
        e = [epi[:, i, :] for i in range(6)]

        adj_loaded = [sem(f"adj_loaded{c}") for c in range(CHUNKS)]
        adj_used = sem("adj_used")
        params_loaded = sem("params_loaded")
        feats_loaded = sem("feats_loaded")
        consts_ready = sem("consts_ready")
        bias_ready = sem("bias_ready")
        agg_copied = sem("agg_copied")
        mm_done = sem("mm_done")
        act_part = sem("act_part")
        dve_part = sem("dve_part")
        gate_lin = sem("gate_lin")
        gate_new = sem("gate_new")
        gate_rz = sem("gate_rz")
        ln_out = sem("ln_out")
        w_copied = sem("w_copied")
        top_copied = sem("top_copied")
        small_asked, small_done = sem("small_asked"), sem("small_done")
        nodes_ready = sem("nodes_ready")
        hidden_lin = sem("hidden_lin")
        max_ready, max_turned = sem("max_ready"), sem("max_turned")
        maxcol_ready, maxrow_ready = sem("maxcol_ready"), sem("maxrow_ready")
        shifted = sem("shifted")
        probs_ready = sem("probs_ready")
        out_ready, out_stored = sem("out_ready"), sem("out_stored")
        dve_steps, pool_steps = sem("dve_steps"), sem("pool_steps")

        SLOTS = {GRU: 5, HYPER: 1, ATTN: 1}

        def mm_before(p, b):
            per = [SLOTS.get(k, 3) for k in range(PASSES)]
            return b * per[p] + sum(per[:p]) * BLOCKS

        block = ctx.enter_context(nc.Block())

        @block.sync
        def _(sp):
            sp.dma_start(w[:, :, :], weights).then_inc(params_loaded, 16)
            sp.dma_start(cols[:, :], columns).then_inc(params_loaded, 16)
            sp.dma_start(brow[:, :, :].rearrange("p r f -> p (r f)"),
                         rows.to_broadcast([P, R_ALL * F])).then_inc(params_loaded, 16)

            def load(g, b, c, first=False):
                if not first:
                    sp.wait_ge(adj_used, (g - 1) * CHUNKS + c + 1)
                sp.dma_start(ring[:, c, :, :], adj[b, c]).then_inc(adj_loaded[c], 16)

            sp.dma_start(x_in[:, 0:QT, :], x_nodes[:, 0:QT, :]).then_inc(feats_loaded, 16)
            for c in range(CHUNKS):
                load(0, 0, c, first=True)
                if c == 0:
                    sp.dma_start(x_in[:, QT:, :], x_nodes[:, QT:, :]).then_inc(feats_loaded, 16)
            sp.dma_start(xT[:, :], x_feats).then_inc(feats_loaded, 16)
            for p in range(PASSES):
                with sp.Fori(0 if p else 1, BLOCKS) as b:
                    for c in range(CHUNKS):
                        load(b + p * BLOCKS, b, c)
            sp.wait_ge(out_stored, 16 * BLOCKS)

        @block.gpsimd
        def _(pool):
            steps = Steps(pool, pool_steps)
            steps.then(nc.gpsimd.memset(ident[:, :], 0.0))
            nc.gpsimd.affine_select(out=ident[:, :], in_=ident[:, :], compare_op=ALU.not_equal,
                                    fill=1.0, base=0, pattern=[[-1, P]],
                                    channel_multiplier=1).then_inc(consts_ready, 1)
            nc.gpsimd.memset(ones[:, :], 1.0).then_inc(consts_ready, 1)

            def store(b):
                pool.wait_ge(out_ready, b + 1)
                nc.gpsimd.dma_start(out[:, bass.ds(b * QT, QT), :],
                                    top_part[:, bass.ds(b * QT, QT), :]).then_inc(out_stored, 16)

            with pool.Fori(0, BLOCKS) as b:
                store(b)

        @block.tensor
        def _(pe):
            def mm(o, lhsT, rhs, start=True, stop=True):
                return nc.tensor.matmul(o, lhsT, rhs, start=start, stop=stop)

            def weight(k):
                return w[:, k, :]

            def gru_msg(b):
                pe.wait_ge(agg_copied, b + 1)
                mm(e[0][:, :], weight(W_MSG), aggT[:, :]).then_inc(mm_done, 1)

            def gru_gates(b):
                pe.wait_ge(act_part, b * 2 + 1)
                feats = xT[:, bass.ds(b * BW, BW)]
                for g in range(2):
                    mm(e[1 + g][:, :], weight(W_IH + g), t[0][:, :], stop=False)
                    mm(e[1 + g][:, :], weight(W_HH + g), feats, start=False)
                mm(e[3][:, :], weight(W_IH + 2), t[0][:, :])
                mm(e[4][:, :], weight(W_HH + 2), feats).then_inc(mm_done, 1)

            def to_nodes(dst, src, done):
                for q in range(QT):
                    last = nc.tensor.transpose(dst[:, q * P:(q + 1) * P],
                                               src[:, q * P:(q + 1) * P], ident[:, :])
                last.then_inc(done, 1)

            def gru_turn(b):
                pe.wait_ge(dve_part, b + 1)
                to_nodes(e[5], t[3], mm_done)

            def gru_turn_back(b):
                pe.wait_ge(ln_out, b + 1)
                to_nodes(e[0], t[4], mm_done)

            def gru_embed(b):
                pe.wait_ge(act_part, b * 2 + 2)
                for k, o in ((W_EMBED, e[1]), (W_TOP, e[2])):
                    for q in range(QT):
                        s = slice(q * P, (q + 1) * P)
                        last = mm(o[:, s], t[5][:, s], weight(k))
                last.then_inc(mm_done, 1)

            def hyper_out(b):
                pe.wait_ge(agg_copied, b + (BLOCKS + 1))
                for q in range(QT):
                    s = slice(q * P, (q + 1) * P)
                    mm(e[0][:, s], aggT[:, s], weight(W_BOT))
                for q in range(QT):
                    last = mm(e[1][:, q:q + 1], sqT[:, q * P:(q + 1) * P], ones[:, 0:1])
                last.then_inc(mm_done, 1)

            def attn_turn(b):
                pe.wait_ge(agg_copied, b + (ATTN * BLOCKS + 1))
                to_nodes(e[4], t[0], mm_done)

            def mlp_slots(r):
                k = (W_UV, W_VU)[r % 2]
                n = r * BLOCKS

                def first(b):
                    pe.wait_ge(agg_copied, b + (MLP0 * BLOCKS + n + 1))
                    mm(e[0][:, :], weight(k), aggT[:, :]).then_inc(mm_done, 1)

                def second(b):
                    pe.wait_ge(dve_part, 2 * b + (BLOCKS + 2 * n + 1))
                    mm(e[1][:, :], weight(k + 1), t[0][:, :]).then_inc(mm_done, 1)

                def third(b):
                    pe.wait_ge(dve_part, 2 * b + (BLOCKS + 2 * n + 2))
                    for q in range(QT):
                        s = slice(q * P, (q + 1) * P)
                        last = mm(e[2][:, s], t[1][:, s], weight(k + 2))
                    last.then_inc(mm_done, 1)

                return {0: first, 2: second, 4: third}

            slots = [{0: gru_msg, 1: gru_gates, 3: gru_turn, 5: gru_turn_back, 6: gru_embed},
                     {0: hyper_out}, {1: attn_turn}]
            slots += [mlp_slots(r) for r in range(ROUNDS)]

            def run_slot(p, b, c):
                if c in slots[p]:
                    slots[p][c](b)

            def aggregate(p, value, b, bank, before, first=False):
                g = b + p * BLOCKS
                for c in range(CHUNKS):
                    if p and first:
                        pe.wait_ge(nodes_ready, (p - 1) * BLOCKS + c + 1)
                    pe.wait_ge(adj_loaded[c], g * 16 + 16)
                    for q in range(QT):
                        j = c * QT + q
                        last = mm(acc[:, bank, :], value[:, j, :], ring[:, c, q, :],
                                  start=j == 0, stop=j == TILES - 1)
                    last.then_inc(adj_used, 1)
                    if before:
                        run_slot(*before, c)

            def attend(b, bank, before):
                pe.wait_ge(max_ready, b + 1)
                to_nodes(e[2], mx[:, 0, :], max_turned)
                pe.wait_ge(maxcol_ready, b + 1)
                to_nodes(e[3], t[1], maxrow_ready)
                for c in range(CHUNKS):
                    pe.wait_ge(probs_ready, b * CHUNKS + (c + 1))
                    for q in range(QT):
                        j = c * QT + q
                        flags = dict(start=j == 0, stop=j == TILES - 1)
                        mm(acc[:, bank, :], x_hyper[:, j, :], ring[:, c, q, :], **flags)
                        last = mm(e[bank][:, :], ones[:, :], ring[:, c, q, :], **flags)
                    last.then_inc(adj_used, 1)
                    if before:
                        run_slot(*before, c)

            pe.wait_ge(params_loaded, 48)
            pe.wait_ge(consts_ready, 2)
            pe.wait_ge(feats_loaded, 48)
            for p in range(PASSES):
                value = [x_in, lifted, x_hyper, *rounds][p]

                def one(b, bank, before, first=False):
                    if p == ATTN:
                        attend(b, bank, before)
                    else:
                        aggregate(p, value, b, bank, before, first)

                if p == ATTN:
                    for c in range(CHUNKS):
                        run_slot(HYPER, BLOCKS - 1, c)
                    one(0, 0, None)
                else:
                    one(0, 0, (p - 1, BLOCKS - 1) if p else None, first=True)
                with pe.Fori(0, (BLOCKS - 2) // 2) as i:
                    for k in (1, 2):
                        one(i * 2 + k, k % 2, (p, i * 2 + (k - 1)))
                one(BLOCKS - 1, (BLOCKS - 1) % 2, (p, BLOCKS - 2))
            for c in range(CHUNKS):
                run_slot(PASSES - 1, BLOCKS - 1, c)

        @block.scalar
        def _(act):
            def aggregated(p, b):
                act.wait_ge(adj_used, (b + p * BLOCKS) * CHUNKS + CHUNKS)

            def temps_free(p, b):
                if 0 < p < PASSES - 1:
                    act.wait_ge(nodes_ready, b + p * BLOCKS)
                elif not isinstance(b, int):
                    act.wait_ge(nodes_ready if p == 0 else out_ready, b)

            def small(layer, b, k, func):
                act.wait_ge(small_asked, small_before(layer, b) + k)
                nc.scalar.activation(s_out[:, :], s_in[:, :], func).then_inc(small_done, 1)

            def gru(b):
                aggregated(GRU, b)
                nc.scalar.activation(aggT[:, :], acc[:, b % 2, :], ACT.Copy).then_inc(agg_copied, 1)
                temps_free(GRU, b)
                act.wait_ge(mm_done, mm_before(GRU, b) + 1)
                nc.scalar.activation(t[0][:, :], e[0][:, :], ACT.Relu,
                                     bias=cols[:, C_MSG:C_MSG + 1]).then_inc(act_part, 1)
                act.wait_ge(mm_done, mm_before(GRU, b) + 2)
                for g in range(2):
                    last = nc.scalar.activation(t[1 + g][:, :], e[1 + g][:, :], ACT.Sigmoid,
                                                bias=bias_rz[:, g:g + 1])
                last.then_inc(gate_rz, 1)
                act.wait_ge(gate_lin, b + 1)
                nc.scalar.activation(t[3][:, :], t[1][:, :], ACT.Tanh,
                                     bias=cols[:, C_IH + 2:C_IH + 3]).then_inc(gate_new, 1)
                small(GRU, b, 1, ACT.Sqrt)
                act.wait_ge(ln_out, b + 1)
                nc.scalar.activation(x_gru[:, bass.ds(b * QT, QT), :].rearrange("p q f -> p (q f)"),
                                     t[4][:, :], ACT.Copy)
                act.wait_ge(mm_done, mm_before(GRU, b) + 4)
                nc.scalar.activation(t[5][:, :], e[0][:, :], ACT.Copy).then_inc(act_part, 1)
                act.wait_ge(mm_done, mm_before(GRU, b) + 5)
                nc.scalar.activation(t[0][:, :], e[1][:, :], ACT.Copy).then_inc(w_copied, 1)
                nc.scalar.activation(top_part[:, bass.ds(b * QT, QT), :].rearrange("p q f -> p (q f)"),
                                     e[2][:, :], ACT.Copy).then_inc(top_copied, 1)
                for k, func in enumerate((ACT.Sqrt, ACT.Ln, ACT.Tanh, ACT.Sqrt, ACT.Ln)):
                    small(GRU, b, k + 2, func)

            def hyper(b):
                aggregated(HYPER, b)
                nc.scalar.activation(aggT[:, :], acc[:, b % 2, :], ACT.Copy)
                nc.scalar.activation(sqT[:, :], acc[:, b % 2, :], ACT.Square).then_inc(agg_copied, 1)
                for k, func in enumerate((ACT.Sqrt, ACT.Tanh, ACT.Sqrt, ACT.Ln, ACT.Tanh, ACT.Sqrt)):
                    small(HYPER, b, k + 1, func)

            def attn(b, before=None):
                for c in range(CHUNKS):
                    act.wait_ge(shifted, b * CHUNKS + (c + 1))
                    nc.scalar.activation(ring[:, c, :, :], ring[:, c, :, :],
                                         ACT.Exp).then_inc(probs_ready, 1)
                    if c == 4 and before is not None:
                        small(ATTN, before, 1, ACT.Sqrt)

            def mlp(r, b):
                p = MLP0 + r
                aggregated(p, b)
                nc.scalar.activation(aggT[:, :], acc[:, b % 2, :], ACT.Copy).then_inc(agg_copied, 1)
                temps_free(p, b)
                for k in range(2):
                    act.wait_ge(mm_done, mm_before(p, b) + (k + 1))
                    c = (C_UV, C_VU)[r % 2] + k
                    nc.scalar.activation(t[2 + k][:, :], e[k][:, :], ACT.Identity,
                                         bias=cols[:, c:c + 1]).then_inc(hidden_lin, 1)
                if p == PASSES - 1:
                    small(p, b, 1, ACT.Sqrt)

            act.wait_ge(params_loaded, 48)
            act.wait_ge(bias_ready, 1)
            gru(0)
            with act.Fori(1, BLOCKS) as b:
                gru(b)
            with act.Fori(0, BLOCKS) as b:
                hyper(b)
            attn(0)
            with act.Fori(1, BLOCKS) as b:
                attn(b, b - 1)
            small(ATTN, BLOCKS - 1, 1, ACT.Sqrt)
            for r in range(ROUNDS - 1):
                with act.Fori(0, BLOCKS) as b:
                    mlp(r, b)
            mlp(ROUNDS - 1, 0)
            with act.Fori(1, BLOCKS) as b:
                mlp(ROUNDS - 1, b)

        @block.vector
        def _(dve):
            v = nc.vector
            steps = Steps(dve, dve_steps)
            then = steps.then
            row = [sc[:, k, :] for k in range(24)]
            A, B, C, R, Q = row[:5]
            HALF = slice(0, QT)
            REST = slice(QT, 2 * QT)

            def at(buffer, b):
                return buffer[:, bass.ds(b * QT, QT), :]

            def tiles(x):
                return x[:, :].rearrange("p (q f) -> p q f", q=QT)

            def per_row(x):
                return x.unsqueeze(2).to_broadcast([P, QT, F])

            def per_feature(k):
                return brow[:, k, :].unsqueeze(1).to_broadcast([P, QT, F])

            def tt(o, a, b, op):
                return v.tensor_tensor(o, a, b, op)

            def ts(o, a, s1, s2, op0, op1=None):
                return v.tensor_scalar(o, a, s1, s2, op0, *([op1] if op1 is not None else []))

            def stt(o, a, s, b, op0, op1):
                return v.scalar_tensor_tensor(o, a, s, b, op0, op1)

            def ask(layer, b, k, instruction):
                instruction.then_inc(small_asked, 1)
                dve.wait_ge(small_done, small_before(layer, b) + k)

            def layernorm(y, o, layer, b, k, done):
                for q in range(QT):
                    last = v.bn_stats(stats[:, q, :], y[:, q, :])
                then(last)
                for q in range(QT):
                    last = v.bn_aggr(mv[:, q, :], stats[:, q, :])
                then(last)
                ask(layer, b, k, ts(s_in[:, HALF], mv[:, :, 1], LN_EPS, None, ALU.add))
                then(v.reciprocal(row[5], s_out[:, HALF]))
                for q in range(QT):
                    last = ts(o[:, q, :], y[:, q, :], mv[:, q, 0:1], row[5][:, q:q + 1],
                              ALU.subtract, ALU.mult)
                done(last)

            def atanh_over(n, o, layer, b, k):
                c, u, lg, small, sq, near = row[6:12]
                then(ts(c, n, MAX_TANH, None, ALU.min))
                ts(u, c, -1.0, 1.0, ALU.mult, ALU.add)
                then(tt(sq, c, c, ALU.mult))
                then(v.reciprocal(u, u))
                ask(layer, b, k, stt(s_in[:, HALF], c, 1.0, u, ALU.add, ALU.mult))
                then(ts(small, sq, 1 / 9, 1 / 7, ALU.mult, ALU.add))
                for term in (1 / 5, 1 / 3, 1.0):
                    then(tt(small, small, sq, ALU.mult))
                    then(ts(small, small, term, None, ALU.add))
                then(tt(small, small, c, ALU.mult))
                then(ts(lg, s_out[:, HALF], 0.5, None, ALU.mult))
                then(tt(small, small, lg, ALU.subtract))
                then(ts(near, c, 0.125, None, ALU.is_lt))
                then(tt(small, small, near, ALU.mult))
                then(tt(lg, lg, small, ALU.add))
                then(v.reciprocal(u, n))
                then(tt(o, lg, u, ALU.mult))

            def mobius(y, root, bias, layer, b, k):
                nu, th, x2, xy, den = row[12:17]
                then(tt(nu, C, root, ALU.mult))
                then(ts(nu, nu, EPS, None, ALU.max))
                ask(layer, b, k, v.tensor_copy(s_in[:, HALF], nu))
                then(v.reciprocal(nu, nu))
                then(tt(th, s_out[:, HALF], C, ALU.mult))
                then(tt(th, th, nu, ALU.mult))
                then(tt(x2, th, th, ALU.mult))
                then(tt(x2, x2, Q, ALU.mult))
                then(stt(xy, th, 2.0, R, ALU.mult, ALU.mult))
                then(ts(xy, xy, 1.0, None, ALU.add))
                then(stt(den, x2, bias_sq[:, bias:bias + 1], xy, ALU.mult, ALU.add))
                then(ts(den, den, EPS, None, ALU.max))
                then(v.reciprocal(den, den))
                then(ts(xy, xy, bias_sq[:, bias:bias + 1], None, ALU.add))
                then(tt(xy, xy, th, ALU.mult))
                then(tt(A, xy, den, ALU.mult))
                then(ts(x2, x2, -1.0, 1.0, ALU.mult, ALU.add))
                then(tt(B, x2, den, ALU.mult))

            def moved(y, o, scratch, bias):
                tt(tiles(o), tiles(y), per_row(A), ALU.mult)
                then(tt(tiles(scratch), per_feature(bias), per_row(B), ALU.mult))
                then(tt(o[:, :], o[:, :], scratch[:, :], ALU.add))

            def gru(b):
                feats = xT[:, bass.ds(b * BW, BW)]
                dve.wait_ge(gate_rz, b + 1)
                then(stt(t[1][:, :], e[4][:, :], cols[:, C_HH + 2:C_HH + 3], t[1][:, :],
                         ALU.add, ALU.mult))
                tt(t[1][:, :], t[1][:, :], e[3][:, :], ALU.add).then_inc(gate_lin, 1)
                dve.wait_ge(gate_new, b + 1)
                then(tt(t[1][:, :], feats, t[3][:, :], ALU.subtract))
                then(tt(t[1][:, :], t[1][:, :], t[2][:, :], ALU.mult))
                then(tt(t[1][:, :], t[1][:, :], t[3][:, :], ALU.add))
                tt(t[3][:, :], feats, t[1][:, :], ALU.add).then_inc(dve_part, 1)
                dve.wait_ge(mm_done, mm_before(GRU, b) + 3)
                layernorm(tiles(e[5]), tiles(t[4]), GRU, b, 1, lambda i: i.then_inc(ln_out, 1))
                dve.wait_ge(w_copied, b + 1)
                dve.wait_ge(ln_out, b + 1)
                tt(t[5][:, :], t[4][:, :], t[4][:, :], ALU.mult)
                tt(t[2][:, :], t[0][:, :], t[0][:, :], ALU.mult)
                then(tt(tiles(t[3]), tiles(t[0]), per_feature(R_EMBED), ALU.mult))
                v.tensor_reduce(s_in[:, HALF], tiles(t[5]), AX.X, ALU.add)
                v.tensor_reduce(R, tiles(t[3]), AX.X, ALU.add)
                then(v.tensor_reduce(Q, tiles(t[2]), AX.X, ALU.add))
                v.tensor_copy(x_sq[:, bass.ds(b * QT, QT)], s_in[:, HALF])
                ask(GRU, b, 2, v.tensor_copy(s_in[:, REST], Q))
                norm, root = row[17], row[18]
                ts(norm, s_out[:, HALF], EPS, None, ALU.max)
                then(v.tensor_copy(root, s_out[:, REST]))
                atanh_over(norm, C, GRU, b, 3)
                mobius(t[0], root, 0, GRU, b, 4)
                moved(t[0], t[1], t[2], R_EMBED)
                then(tt(t[2][:, :], t[1][:, :], t[1][:, :], ALU.mult))
                v.tensor_reduce(s_in[:, HALF], tiles(t[2]), AX.X, ALU.add).then_inc(small_asked, 1)
                dve.wait_ge(small_done, small_before(GRU, b) + 5)
                then(ts(norm, s_out[:, HALF], EPS, None, ALU.max))
                atanh_over(norm, C, GRU, b, 6)
                tt(at(lifted, b), tiles(t[1]), per_row(C), ALU.mult).then_inc(nodes_ready, 1)

            def hyper(b):
                dve.wait_ge(mm_done, mm_before(HYPER, b) + 1)
                qa, na, beta, root = row[17], row[18], row[19], row[20]
                v.tensor_copy(qa, e[1][:, 0:QT])
                ask(HYPER, b, 1, v.tensor_copy(s_in[:, HALF], e[1][:, 0:QT]))
                then(ts(na, s_out[:, HALF], EPS, None, ALU.max))
                ask(HYPER, b, 2, v.tensor_copy(s_in[:, HALF], na))
                then(v.reciprocal(na, na))
                then(tt(beta, s_out[:, HALF], na, ALU.mult))
                tt(tiles(t[0]), tiles(e[0]), per_row(beta), ALU.mult)
                then(tt(qa, qa, beta, ALU.mult))
                dve.wait_ge(top_copied, b + 1)
                tt(tiles(t[0]), tiles(t[0]), at(top_part, b), ALU.add)
                then(tt(qa, qa, beta, ALU.mult))
                tt(s_in[:, HALF], qa, x_sq[:, bass.ds(b * QT, QT)], ALU.add)
                tt(t[1][:, :], t[0][:, :], t[0][:, :], ALU.mult)
                then(tt(tiles(t[2]), tiles(t[0]), per_feature(R_LAYER), ALU.mult))
                v.tensor_reduce(R, tiles(t[2]), AX.X, ALU.add)
                then(v.tensor_reduce(Q, tiles(t[1]), AX.X, ALU.add))
                ask(HYPER, b, 3, v.tensor_copy(s_in[:, REST], Q))
                ts(na, s_out[:, HALF], EPS, None, ALU.max)
                then(v.tensor_copy(root, s_out[:, REST]))
                atanh_over(na, C, HYPER, b, 4)
                mobius(t[0], root, 1, HYPER, b, 5)
                moved(t[0], t[1], t[2], R_LAYER)
                then(tt(tiles(t[1]), tiles(t[1]), at(x_gru, b), ALU.add))
                layernorm(tiles(t[1]), tiles(t[2]), HYPER, b, 6, then)
                v.tensor_copy(at(x_hyper, b), tiles(t[2]))
                then(tt(tiles(t[3]), tiles(t[2]), per_feature(R_HV), ALU.mult))
                v.tensor_reduce(score[:, bass.ds(b * QT, QT)], tiles(t[3]), AX.X,
                                ALU.add).then_inc(nodes_ready, 1)

            def logits(b, c):
                dve.wait_ge(adj_loaded[c], b * 16 + (ATTN * BLOCKS + 1) * 16)
                chunk = ring[:, c, :, :]
                then(ts(big[:, :, :], chunk, 0.0, NEG, ALU.is_equal, ALU.mult))
                for q in range(QT):
                    j = c * QT + q
                    last = stt(ring[:, c, q, :], ring[:, c, q, :], score[:, j:j + 1], big[:, q, :],
                               ALU.mult, ALU.add)
                then(last)
                if c == 0:
                    then(v.tensor_copy(mx[:, :, :], chunk))
                else:
                    then(tt(mx[:, :, :], mx[:, :, :], chunk, ALU.max))

            def maxima(b):
                then(tt(mx[:, 0:2, :], mx[:, 0:2, :], mx[:, 2:4, :], ALU.max))
                tt(mx[:, 0, :], mx[:, 0, :], mx[:, 1, :], ALU.max).then_inc(max_ready, 1)
                dve.wait_ge(max_turned, b + 1)
                then(v.tensor_reduce(row[0], tiles(e[2]), AX.X, ALU.max))
                v.tensor_copy(tiles(t[1]), per_row(row[0])).then_inc(maxcol_ready, 1)
                dve.wait_ge(maxrow_ready, b + 1)
                then(ts(valid[:, b % 2, :], e[3][:, :], NEG, None, ALU.is_gt))

            def shift(b, c):
                tt(ring[:, c, :, :], ring[:, c, :, :],
                   e[3][:, :].unsqueeze(1).to_broadcast([P, QT, BW]),
                   ALU.subtract).then_inc(shifted, 1)

            def attended(b):
                dve.wait_ge(adj_used, b * CHUNKS + (ATTN * BLOCKS + 1) * CHUNKS)
                then(v.reciprocal(t[2][:, :], epi[:, b % 2, :]))
                then(tt(t[2][:, :], t[2][:, :], valid[:, b % 2, :], ALU.mult))
                tt(t[0][:, :], acc[:, b % 2, :], t[2][:, :], ALU.mult).then_inc(agg_copied, 1)

            def attn_norm(b):
                dve.wait_ge(mm_done, mm_before(ATTN, b) + 1)
                then(tt(tiles(t[3]), tiles(e[4]), at(x_hyper, b), ALU.add))
                layernorm(tiles(t[3]), at(x_attn, b), ATTN, b, 1,
                          lambda i: i.then_inc(nodes_ready, 1))

            def attn(b, before=None, after=None):
                for c in range(CHUNKS):
                    shift(b, c)
                    if before is not None:
                        if c == 1:
                            attended(before)
                        if c == 4:
                            attn_norm(before)
                    if after is not None and c >= 3:
                        logits(after, c - 3)
                if after is not None:
                    for c in range(CHUNKS - 3, CHUNKS):
                        logits(after, c)
                    maxima(after)

            def leaky(o, x):
                return stt(o, x, SLOPE, x, ALU.mult, ALU.max)

            def mlp(r, b):
                p = MLP0 + r
                for k in range(2):
                    dve.wait_ge(hidden_lin, 2 * b + (2 * r * BLOCKS + k + 1))
                    leaky(t[k][:, :], t[2 + k][:, :]).then_inc(dve_part, 1)
                dve.wait_ge(mm_done, mm_before(p, b) + 3)
                then(tt(tiles(t[4]), tiles(e[2]), per_feature((R_UV, R_VU)[r % 2]), ALU.add))
                if p < PASSES - 1:
                    leaky(at(written[r], b), tiles(t[4])).then_inc(nodes_ready, 1)
                else:
                    then(leaky(t[5][:, :], t[4][:, :]))
                    then(tt(tiles(t[5]), tiles(t[5]), at(x_attn, b), ALU.add))
                    layernorm(tiles(t[5]), at(top_part, b), p, b, 1,
                              lambda i: i.then_inc(out_ready, 1))

            dve.wait_ge(params_loaded, 48)
            v.tensor_tensor(bias_rz[:, :], cols[:, C_IH:C_IH + 2], cols[:, C_HH:C_HH + 2], ALU.add)
            v.memset(s_in[:, :], 1.0)
            for k, r in enumerate((R_EMBED, R_LAYER)):
                then(tt(t[k][:, 0:F], brow[:, r, :], brow[:, r, :], ALU.mult))
                last = v.tensor_reduce(bias_sq[:, k:k + 1], t[k][:, 0:F], AX.X, ALU.add)
            last.then_inc(bias_ready, 1)
            dve.wait_ge(bias_ready, 1)
            dve.wait_ge(feats_loaded, 48)
            with dve.Fori(0, BLOCKS) as b:
                steps.restart()
                gru(b)
            with dve.Fori(0, BLOCKS) as b:
                steps.restart()
                hyper(b)
            dve.wait_ge(nodes_ready, (HYPER + 1) * BLOCKS)
            steps.restart()
            for c in range(CHUNKS):
                logits(0, c)
            maxima(0)
            attn(0, after=1)
            with dve.Fori(1, BLOCKS - 1) as b:
                steps.restart()
                attn(b, b - 1, b + 1)
            steps.restart()
            attn(BLOCKS - 1, BLOCKS - 2)
            attended(BLOCKS - 1)
            attn_norm(BLOCKS - 1)
            for r in range(ROUNDS):
                with dve.Fori(0, BLOCKS) as b:
                    steps.restart()
                    mlp(r, b)


def kernel(x, adj, L0_gnn_W_msg, L0_gnn_b_msg, L0_gnn_W_ih, L0_gnn_W_hh, L0_gnn_b_ih, L0_gnn_b_hh,
           L1_gnn_embed, L1_gnn_layer, L1_gnn_embed_bias, L1_gnn_layer_bias, L2_gnn_H_v,
           L3_gnn_v_node_feats, L3_gnn_uv_W1, L3_gnn_uv_b1, L3_gnn_uv_W2, L3_gnn_uv_b2,
           L3_gnn_uv_W3, L3_gnn_uv_b3, L3_gnn_vu_W1, L3_gnn_vu_b1, L3_gnn_vu_W2, L3_gnn_vu_b2,
           L3_gnn_vu_W3, L3_gnn_vu_b3):
    import numpy as np
    import concourse.bacc as bacc
    from concourse.bass_utils import run_bass_kernel_spmd

    def a(v):
        return np.asarray(v)

    adj_blocks = a(adj).reshape(BLOCKS, BW, CHUNKS, QT, P).transpose(0, 2, 4, 3, 1)
    xs = a(x)
    weights = np.concatenate(
        [a(L0_gnn_W_msg).T, a(L0_gnn_W_ih).T, a(L0_gnn_W_hh).T, a(L1_gnn_embed),
         a(L1_gnn_layer)[:F], a(L1_gnn_layer)[F:], a(L3_gnn_uv_W1), a(L3_gnn_uv_W2),
         a(L3_gnn_uv_W3), a(L3_gnn_vu_W1), a(L3_gnn_vu_W2), a(L3_gnn_vu_W3)], axis=1)
    columns = np.stack(
        [a(L0_gnn_b_msg), *a(L0_gnn_b_ih).reshape(3, F), *a(L0_gnn_b_hh).reshape(3, F),
         a(L3_gnn_uv_b1), a(L3_gnn_uv_b2), a(L3_gnn_vu_b1), a(L3_gnn_vu_b2)], axis=1)
    rows = np.concatenate([a(L1_gnn_embed_bias), a(L1_gnn_layer_bias), a(L2_gnn_H_v)[:, 0],
                           a(L3_gnn_uv_b3), a(L3_gnn_vu_b3)])[None, :]
    arrays = {
        "adj": adj_blocks, "x_nodes": xs.reshape(TILES, P, F).transpose(1, 0, 2),
        "x_feats": xs.T, "weights": weights.reshape(F, W_ALL, P), "columns": columns, "rows": rows,
    }
    arrays = {f"in_{k}": np.ascontiguousarray(v) for k, v in arrays.items()}
    nc = bacc.Bacc("TRN2", target_bir_lowering=False, num_devices=1)
    args = [nc.dram_tensor(k, v.shape, FP32, kind="ExternalInput").ap() for k, v in arrays.items()]
    args.append(nc.dram_tensor("out", (P, TILES, F), FP32, kind="ExternalOutput").ap())
    build(nc, *args)
    r = run_bass_kernel_spmd(nc, [arrays], core_ids=[0])
    return np.ascontiguousarray(np.asarray(r.results[0]["out"]).transpose(1, 0, 2)).reshape(N, F)
```

```python
import concourse.bass as bass
from concourse import mybir
from contextlib import ExitStack

FP32 = mybir.dt.float32
FP32R = mybir.dt.float32r
ALU = mybir.AluOpType
ACT = mybir.ActivationFunctionType
AX = mybir.AxisListType

N, F = 4096, 128
P = 128
TILES = N // P
BW = 512
BLOCKS = N // BW
QT = BW // P
CHUNKS = TILES // QT
NEG = -1e9
EPS = 1e-7
MAX_TANH = 1.0 - 1e-6
LN_EPS = 1e-5
SLOPE = 0.01

GRU, HYPER, ATTN, MLP0, ROUNDS = 0, 1, 2, 3, 5
PASSES = MLP0 + ROUNDS
SMALL = {GRU: 6, HYPER: 6, ATTN: 1}
GROUPS, TURN_BUFS, TURN_LEAD = TILES // QT, 4, 2
HALF_ROW = N // 2
LOWEST = -3.0e38
HALF_QT, PART_BUFS = QT // 2, 4
ACT_STAGES, DVE_STAGES = {1: 0, 2: 1, 4: 2, 6: 3}, {2: 0, 4: 1, 6: 2}

(W_MSG, W_IH, W_HH, W_EMBED, W_TOP, W_BOT, W_UV, W_VU, W_ALL) = (0, 1, 4, 7, 8, 9, 10, 13, 16)
(C_MSG, C_IH, C_HH, C_UV, C_VU, C_ALL) = (0, 1, 4, 7, 9, 11)
R_EMBED, R_LAYER, R_HV, R_UV, R_VU, R_ALL = range(6)


class Steps:

    def __init__(self, engine, sem):
        self.engine, self.sem, self.n = engine, sem, 0

    def count(self, instruction):
        self.n += 1
        instruction.then_inc(self.sem, 1)

    def wait(self):
        self.engine.wait_ge(self.sem, self.n)

    def then(self, instruction):
        self.count(instruction)
        self.wait()

    def restart(self):
        self.engine.sem_clear(self.sem)
        self.n = 0


def small_before(layer, b):
    at = {GRU: 0, HYPER: SMALL[GRU] * BLOCKS, ATTN: (SMALL[GRU] + SMALL[HYPER]) * BLOCKS,
          PASSES - 1: (SMALL[GRU] + SMALL[HYPER] + SMALL[ATTN]) * BLOCKS}[layer]
    return b * SMALL.get(layer, 1) + at


def gru_norm_ask(b):
    return 1 if isinstance(b, int) and b == 0 else b * SMALL[GRU]


def lift_ask(b, k):
    last = isinstance(b, int) and b == BLOCKS - 1
    return b * SMALL[GRU] + (1 + k + (k == 5 and not last))


def build(nc, adj, adj_rows, x_nodes, x_feats, weights, columns, rows, out):
    with ExitStack() as ctx:
        def sb(name, *shape):
            return ctx.enter_context(nc.sbuf_tensor(name, [P, *shape], FP32))

        def sem(name):
            return ctx.enter_context(nc.semaphore(name))

        ring = sb("ring", CHUNKS, QT, BW)
        def sb_at(name, *shape):
            tensor = sb(name, *shape)
            size = 4
            for n in shape:
                size *= n
            return tensor, nc.sbuf_base - size

        x_in, x_in_at = sb_at("x_in", TILES, F)
        x_gru, x_gru_at = sb_at("x_gru", TILES, F)
        x_hyper = x_gru
        lifted = sb("lifted", TILES, F)
        x_attn = lifted
        top_part, top_part_at = sb_at("top_part", TILES, F)
        xT, xT_at = sb_at("xT", N)
        work, work_at = sb_at("work", 4, HALF_ROW)
        def over(name, offset, *shape):
            return nc.alloc_sbuf_tensor_at(name, [P, *shape], FP32R, offset=offset)

        split = [(over("value_hi0", x_in_at, TILES, F), over("value_lo0", top_part_at, TILES, F)),
                 (over("value_hi1", x_gru_at, TILES, F), over("value_lo1", xT_at, TILES, F))]
        part_size = 4 * HALF_QT * BW
        lift = [work[:, i, 0:BW] for i in range(4)]
        adj_hi = [over(f"adj_hi{i}", work_at + i * part_size, HALF_QT, BW)
                  for i in range(PART_BUFS)]
        adj_lo = [over(f"adj_lo{i}", work_at + (PART_BUFS + i) * part_size, HALF_QT, BW)
                  for i in range(PART_BUFS)]
        result = x_gru
        w = sb("w", W_ALL, P)
        cols = sb("cols", C_ALL)
        bias_rz = sb("bias_rz", 2)
        brow = sb("brow", R_ALL, F)
        ident = sb("ident", P)
        ones = sb("ones", P)
        x_sq = sb("x_sq", TILES)
        bias_sq = sb("bias_sq", 2)
        aggT = sb("aggT", BW)
        sqT = sb("sqT", BW)
        t = [sb(f"t{i}", BW) for i in range(6)]
        score_row = xT
        mask = work[:, 0:2, :]
        turned = [work[:, 2 + i // QT, (i % QT) * BW:(i % QT + 1) * BW] for i in range(TURN_BUFS)]
        half_max = sb("half_max", 2)
        row_max = sb("row_max", 2, QT)
        minus_max = sb("minus_max", QT)
        half_sum = sb("half_sum", 2, 2, QT)
        stats = sb("stats", QT, 6)
        mv = sb("mv", QT, 2)
        s_in = sb("s_in", 2 * QT)
        s_out = sb("s_out", 2 * QT)
        sc = sb("sc", 24, QT)

        acc = ctx.enter_context(nc.psum_tensor("acc", [P, 2, BW], FP32))
        epi = ctx.enter_context(nc.psum_tensor("epi", [P, 6, BW], FP32))
        e = [epi[:, i, :] for i in range(6)]

        adj_loaded = [sem(f"adj_loaded{c}") for c in range(CHUNKS)]
        adj_used = sem("adj_used")
        params_loaded = sem("params_loaded")
        first_nodes_loaded, nodes_loaded = sem("first_nodes_loaded"), sem("nodes_loaded")
        feats_loaded = sem("feats_loaded")
        consts_ready = sem("consts_ready")
        bias_ready = sem("bias_ready")
        agg_copied = sem("agg_copied")
        mm_done = sem("mm_done")
        act_part = sem("act_part")
        dve_part = sem("dve_part")
        gate_lin = sem("gate_lin")
        gate_new = sem("gate_new")
        gate_rz = sem("gate_rz")
        ln_out = sem("ln_out")
        w_copied = sem("w_copied")
        top_copied = sem("top_copied")
        small_asked, small_done = sem("small_asked"), sem("small_done")
        nodes_ready = sem("nodes_ready")
        hidden_lin = sem("hidden_lin")
        score_ready = sem("score_ready")
        masked = sem("masked")
        scaled = sem("scaled")
        logits_ready = sem("logits_ready")
        probs_ready = sem("probs_ready")
        probs_turned = sem("probs_turned")
        turn_copied = sem("turn_copied")
        hi_ready = sem("hi_ready")
        lo_ready = sem("lo_ready")
        out_ready, out_stored = sem("out_ready"), sem("out_stored")
        dve_steps, pool_steps = sem("dve_steps"), sem("pool_steps")

        SLOTS = {GRU: 5, HYPER: 2, ATTN: 0}

        def mm_before(p, b):
            per = [SLOTS.get(k, 3) for k in range(PASSES)]
            return b * per[p] + sum(per[:p]) * BLOCKS

        block = ctx.enter_context(nc.Block())

        @block.sync
        def _(sp):
            def load(g, b, c, first=False):
                if not first:
                    sp.wait_ge(adj_used, (g - 1) * CHUNKS + c + 1)
                sp.dma_start(ring[:, c, :, :], adj[b, c]).then_inc(adj_loaded[c], 16)

            def load_again(r, b, c):
                sp.wait_ge(lo_ready, ((b + r * BLOCKS - 1) * CHUNKS + c + 1) * 2)
                sp.dma_start(ring[:, c, :, :], adj[b, c]).then_inc(adj_loaded[c], 16)

            def load_rows(g, b, c):
                sp.wait_ge(adj_used, (g - 1) * CHUNKS + c + 1)
                sp.dma_start(ring[:, c, :, :].rearrange("p q w -> p (q w)"),
                             adj_rows[b, c // 2, :, c % 2, :]).then_inc(adj_loaded[c], 16)

            sp.dma_start(x_in[:, 0:QT, :], x_nodes[:, 0:QT, :]).then_inc(first_nodes_loaded, 16)
            for c in range(CHUNKS):
                load(0, 0, c, first=True)
                if c == 0:
                    sp.dma_start(x_in[:, QT:, :], x_nodes[:, QT:, :]).then_inc(nodes_loaded, 16)
                if c == 1:
                    sp.dma_start(w[:, :, :], weights).then_inc(params_loaded, 16)
                    sp.dma_start(cols[:, :], columns).then_inc(params_loaded, 16)
                    sp.dma_start(brow[:, :, :].rearrange("p r f -> p (r f)"),
                                 rows.to_broadcast([P, R_ALL * F])).then_inc(params_loaded, 16)
            sp.dma_start(xT[:, :], x_feats).then_inc(feats_loaded, 16)
            for p in range(MLP0):
                with sp.Fori(0 if p else 1, BLOCKS) as b:
                    for c in range(CHUNKS):
                        (load_rows if p == ATTN else load)(b + p * BLOCKS, b, c)
            for c in range(CHUNKS):
                load(MLP0 * BLOCKS, 0, c)
            for r in range(ROUNDS):
                with sp.Fori(0 if r else 1, BLOCKS) as b:
                    for c in range(CHUNKS):
                        load_again(r, b, c)
            sp.wait_ge(out_stored, 16 * BLOCKS)

        @block.gpsimd
        def _(pool):
            steps = Steps(pool, pool_steps)
            steps.then(nc.gpsimd.memset(ident[:, :], 0.0))
            nc.gpsimd.affine_select(out=ident[:, :], in_=ident[:, :], compare_op=ALU.not_equal,
                                    fill=1.0, base=0, pattern=[[-1, P]],
                                    channel_multiplier=1).then_inc(consts_ready, 1)
            nc.gpsimd.memset(ones[:, :], 1.0).then_inc(consts_ready, 1)

            def store(b):
                pool.wait_ge(out_ready, b + 1)
                nc.gpsimd.dma_start(out[:, bass.ds(b * QT, QT), :],
                                    result[:, bass.ds(b * QT, QT), :]).then_inc(out_stored, 16)

            pool.wait_ge(score_ready, BLOCKS)
            with pool.Fori(0, BLOCKS) as b:
                for k in range(QT):
                    pool.wait_ge(masked, b * QT + (k + 1))
                    half = ring[:, 2 * k + 1, :, :].rearrange("p q w -> p (q w)")
                    nc.gpsimd.tensor_tensor(half, half, score_row[:, HALF_ROW:],
                                            ALU.mult).then_inc(scaled, 1)

            with pool.Fori(0, BLOCKS) as b:
                store(b)

        @block.tensor
        def _(pe):
            def mm(o, lhsT, rhs, start=True, stop=True):
                return nc.tensor.matmul(o, lhsT, rhs, start=start, stop=stop)

            def weight(k):
                return w[:, k, :]

            def gru_msg(b):
                pe.wait_ge(agg_copied, b + 1)
                mm(e[0][:, :], weight(W_MSG), aggT[:, :]).then_inc(mm_done, 1)

            def gru_gates(b):
                pe.wait_ge(act_part, b * 2 + 1)
                feats = xT[:, bass.ds(b * BW, BW)]
                for g in range(2):
                    mm(e[1 + g][:, :], weight(W_IH + g), t[0][:, :], stop=False)
                    mm(e[1 + g][:, :], weight(W_HH + g), feats, start=False)
                mm(e[3][:, :], weight(W_IH + 2), t[0][:, :])
                mm(e[4][:, :], weight(W_HH + 2), feats).then_inc(mm_done, 1)

            def to_nodes(dst, src, done):
                for q in range(QT):
                    last = nc.tensor.transpose(dst[:, q * P:(q + 1) * P],
                                               src[:, q * P:(q + 1) * P], ident[:, :])
                last.then_inc(done, 1)

            def gru_turn(b):
                pe.wait_ge(dve_part, b + 1)
                to_nodes(e[5], t[3], mm_done)

            def gru_turn_back(b):
                pe.wait_ge(ln_out, b + 1)
                to_nodes(e[0], t[4], mm_done)

            def gru_embed(b):
                pe.wait_ge(act_part, b * 2 + 2)
                for k, o in ((W_EMBED, e[1]), (W_TOP, e[2])):
                    for q in range(QT):
                        s = slice(q * P, (q + 1) * P)
                        last = mm(o[:, s], t[5][:, s], weight(k))
                last.then_inc(mm_done, 1)

            def hyper_out(b):
                pe.wait_ge(agg_copied, b + (BLOCKS + 1))
                for q in range(QT):
                    s = slice(q * P, (q + 1) * P)
                    mm(e[0][:, s], aggT[:, s], weight(W_BOT))
                for q in range(QT):
                    last = mm(e[1][:, q:q + 1], sqT[:, q * P:(q + 1) * P], ones[:, 0:1])
                last.then_inc(mm_done, 1)

            def hyper_score(b):
                pe.wait_ge(dve_part, b + (BLOCKS + 1))
                to_nodes(e[2], t[4], mm_done)

            def mlp_slots(r):
                k = (W_UV, W_VU)[r % 2]
                n = r * BLOCKS

                def first(b):
                    pe.wait_ge(agg_copied, b + (MLP0 * BLOCKS + n + 1))
                    mm(e[0][:, :], weight(k), aggT[:, :]).then_inc(mm_done, 1)

                def second(b):
                    pe.wait_ge(dve_part, 2 * b + (2 * BLOCKS + 2 * n + 1))
                    mm(e[1][:, :], weight(k + 1), t[0][:, :]).then_inc(mm_done, 1)

                def third(b):
                    pe.wait_ge(dve_part, 2 * b + (2 * BLOCKS + 2 * n + 2))
                    for q in range(QT):
                        s = slice(q * P, (q + 1) * P)
                        last = mm(e[2][:, s], t[1][:, s], weight(k + 2))
                    last.then_inc(mm_done, 1)

                return {0: first, 2: second, 4: third}

            slots = [{0: gru_msg, 1: gru_gates, 3: gru_turn, 5: gru_turn_back, 6: gru_embed},
                     {1: hyper_out, 7: hyper_score}, {}]
            slots += [mlp_slots(r) for r in range(ROUNDS)]

            def run_slot(p, b, c):
                if c in slots[p]:
                    slots[p][c](b)

            def aggregate(p, value, b, bank, before, first=False):
                g = b + p * BLOCKS
                for c in range(CHUNKS):
                    if first and p:
                        pe.wait_ge(nodes_ready, (p - 1) * BLOCKS + c + 1)
                    elif first and c < 2:
                        pe.wait_ge((first_nodes_loaded, nodes_loaded)[c], 16)
                    pe.wait_ge(adj_loaded[c], g * 16 + 16)
                    for q in range(QT):
                        j = c * QT + q
                        last = mm(acc[:, bank, :], value[:, j, :], ring[:, c, q, :],
                                  start=j == 0, stop=j == TILES - 1)
                    last.then_inc(adj_used, 1)
                    if before:
                        run_slot(*before, c)

            def aggregate_split(r, b, bank, before, first=False):
                g = b + (MLP0 + r) * BLOCKS
                hi, lo = split[r % 2]
                for c in range(CHUNKS):
                    if first:
                        pe.wait_ge(nodes_ready, (MLP0 + r - 1) * BLOCKS + c + 1)
                    for h in range(2):
                        pe.wait_ge(lo_ready, ((b + r * BLOCKS) * CHUNKS + c) * 2 + (h + 1))
                        slot = (2 * c + h) % PART_BUFS
                        for q in range(HALF_QT):
                            j = c * QT + h * HALF_QT + q
                            mm(acc[:, bank, :], hi[:, j, :], adj_hi[slot][:, q, :],
                               start=j == 0, stop=False)
                            mm(acc[:, bank, :], hi[:, j, :], adj_lo[slot][:, q, :],
                               start=False, stop=False)
                            last = mm(acc[:, bank, :], lo[:, j, :], adj_hi[slot][:, q, :],
                                      start=False, stop=j == TILES - 1)
                    last.then_inc(adj_used, 1)
                    if before:
                        run_slot(*before, c)

            def attend(b, bank):
                def turn(k, g):
                    n = k * GROUPS + g
                    if g % (GROUPS // 2) == 0:
                        pe.wait_ge(probs_ready, b * (2 * QT) + (2 * k + 2 * g // GROUPS + 1))
                    if not (first and n < TURN_BUFS):
                        pe.wait_ge(turn_copied, b * (QT * GROUPS) + (n - TURN_BUFS + 1))
                    row = ring[:, 2 * k:2 * k + 2, :, :].rearrange("p c q w -> p (c q w)")
                    for q in range(QT):
                        j = g * QT + q
                        last = nc.tensor.transpose(e[g % TURN_BUFS][:, q * P:(q + 1) * P],
                                                   row[:, j * P:(j + 1) * P], ident[:, :])
                    last.then_inc(probs_turned, 1)

                def aggregate_group(k, g):
                    n = k * GROUPS + g
                    pe.wait_ge(turn_copied, b * (QT * GROUPS) + (n + 1))
                    for q in range(QT):
                        j = g * QT + q
                        last = mm(acc[:, bank, k * P:(k + 1) * P],
                                  turned[g % TURN_BUFS][:, q * P:(q + 1) * P],
                                  x_hyper[:, j, :], start=j == 0, stop=j == TILES - 1)
                    if g % (GROUPS // 2) == GROUPS // 2 - 1:
                        last.then_inc(adj_used, 1)

                first = isinstance(b, int) and b == 0
                every = [(k, g) for k in range(QT) for g in range(GROUPS)]
                for n in range(len(every) + TURN_LEAD):
                    if n < len(every):
                        turn(*every[n])
                    if n >= TURN_LEAD:
                        aggregate_group(*every[n - TURN_LEAD])

            for p in range(PASSES):

                if p == ATTN:
                    for c in range(CHUNKS):
                        run_slot(HYPER, BLOCKS - 1, c)
                    attend(0, 0)
                    with pe.Fori(0, (BLOCKS - 2) // 2) as i:
                        for k in (1, 2):
                            attend(i * 2 + k, k % 2)
                    attend(BLOCKS - 1, (BLOCKS - 1) % 2)
                    continue

                def one(b, bank, before, first=False):
                    if p < ATTN:
                        aggregate(p, (x_in, lifted)[p], b, bank, before, first)
                    else:
                        aggregate_split(p - MLP0, b, bank, before, first)

                one(0, 0, (p - 1, BLOCKS - 1) if p else None, first=True)
                if p == 0:
                    pe.wait_ge(params_loaded, 48)
                    pe.wait_ge(consts_ready, 2)
                    pe.wait_ge(feats_loaded, 16)
                with pe.Fori(0, (BLOCKS - 2) // 2) as i:
                    for k in (1, 2):
                        one(i * 2 + k, k % 2, (p, i * 2 + (k - 1)))
                one(BLOCKS - 1, (BLOCKS - 1) % 2, (p, BLOCKS - 2))
            for c in range(CHUNKS):
                run_slot(PASSES - 1, BLOCKS - 1, c)

        @block.scalar
        def _(act):
            def aggregated(p, b):
                act.wait_ge(adj_used, (b + p * BLOCKS) * CHUNKS + CHUNKS)

            def temps_free(p, b):
                if p < PASSES - 1:
                    act.wait_ge(nodes_ready, b + p * BLOCKS)
                elif not isinstance(b, int):
                    act.wait_ge(out_ready, b)

            def small(n, func):
                act.wait_ge(small_asked, n)
                nc.scalar.activation(s_out[:, :], s_in[:, :], func).then_inc(small_done, 1)

            def gru(b, lifting=None):
                aggregated(GRU, b)
                nc.scalar.activation(aggT[:, :], acc[:, b % 2, :], ACT.Copy).then_inc(agg_copied, 1)
                act.wait_ge(mm_done, mm_before(GRU, b) + 1)
                nc.scalar.activation(t[0][:, :], e[0][:, :], ACT.Relu,
                                     bias=cols[:, C_MSG:C_MSG + 1]).then_inc(act_part, 1)
                if lifting is not None:
                    lift_functions(lifting)
                act.wait_ge(mm_done, mm_before(GRU, b) + 2)
                for g in range(2):
                    last = nc.scalar.activation(t[1 + g][:, :], e[1 + g][:, :], ACT.Sigmoid,
                                                bias=bias_rz[:, g:g + 1])
                last.then_inc(gate_rz, 1)
                act.wait_ge(gate_lin, b + 1)
                nc.scalar.activation(t[3][:, :], t[1][:, :], ACT.Tanh,
                                     bias=cols[:, C_IH + 2:C_IH + 3]).then_inc(gate_new, 1)
                small(gru_norm_ask(b), ACT.Sqrt)
                act.wait_ge(ln_out, b + 1)
                nc.scalar.activation(x_gru[:, bass.ds(b * QT, QT), :].rearrange("p q f -> p (q f)"),
                                     t[4][:, :], ACT.Copy)
                if lifting is not None:
                    small(lift_ask(lifting, 5), ACT.Ln)
                act.wait_ge(mm_done, mm_before(GRU, b) + 4)
                nc.scalar.activation(t[5][:, :], e[0][:, :], ACT.Copy).then_inc(act_part, 1)
                act.wait_ge(mm_done, mm_before(GRU, b) + 5)
                nc.scalar.activation(lift[0], e[1][:, :], ACT.Copy).then_inc(w_copied, 1)
                nc.scalar.activation(top_part[:, bass.ds(b * QT, QT), :].rearrange("p q f -> p (q f)"),
                                     e[2][:, :], ACT.Copy).then_inc(top_copied, 1)

            def lift_functions(b):
                for k, func in enumerate((ACT.Sqrt, ACT.Ln, ACT.Tanh, ACT.Sqrt)):
                    small(lift_ask(b, k + 1), func)

            def hyper(b):
                aggregated(HYPER, b)
                nc.scalar.activation(aggT[:, :], acc[:, b % 2, :], ACT.Copy)
                nc.scalar.activation(sqT[:, :], acc[:, b % 2, :], ACT.Square).then_inc(agg_copied, 1)
                for k, func in enumerate((ACT.Sqrt, ACT.Tanh, ACT.Sqrt, ACT.Ln, ACT.Tanh, ACT.Sqrt)):
                    small(small_before(HYPER, b) + (k + 1), func)
                act.wait_ge(mm_done, mm_before(HYPER, b) + 2)
                nc.scalar.activation(score_row[:, bass.ds(b * BW, BW)], e[2][:, :],
                                     ACT.Copy).then_inc(score_ready, 1)

            def exponentials(b, k, h):
                b, k = (b + 1, 0) if k == QT else (b, k)
                act.wait_ge(logits_ready, b * QT + (k + 1))
                half = ring[:, 2 * k + h, :, :].rearrange("p q w -> p (q w)")
                nc.scalar.activation(half, half, ACT.Exp, bias=minus_max[:, k:k + 1],
                                     accum_out=half_sum[:, b % 2, h, k:k + 1])\
                    .then_inc(probs_ready, 1)

            def attn(b, last=False):
                for k in range(QT):
                    for g in range(GROUPS):
                        act.wait_ge(probs_turned, (b * QT + k) * GROUPS + (g + 1))
                        nc.scalar.activation(turned[g % TURN_BUFS][:, :], e[g % TURN_BUFS][:, :],
                                             ACT.Copy).then_inc(turn_copied, 1)
                        if g in (1, 5) and not (last and k == QT - 1):
                            exponentials(b, k + 1, g // (GROUPS // 2))
                        if (k, g) == (0, 3) and not (isinstance(b, int) and b == 0):
                            small(small_before(ATTN, b - 1) + 1, ACT.Sqrt)

            def mlp(r, b, stage):
                p = MLP0 + r
                if stage == 0:
                    aggregated(p, b)
                    nc.scalar.activation(aggT[:, :], acc[:, b % 2, :],
                                         ACT.Copy).then_inc(agg_copied, 1)
                    temps_free(p, b)
                elif stage < 3:
                    k = stage - 1
                    act.wait_ge(mm_done, mm_before(p, b) + (k + 1))
                    c = (C_UV, C_VU)[r % 2] + k
                    nc.scalar.activation(t[2 + k][:, :], e[k][:, :], ACT.Identity,
                                         bias=cols[:, c:c + 1]).then_inc(hidden_lin, 1)
                elif p == PASSES - 1:
                    small(small_before(p, b) + 1, ACT.Sqrt)

            def round_hi(r, b, before):
                for c in range(CHUNKS):
                    act.wait_ge(adj_loaded[c], b * 16 + ((MLP0 + r) * BLOCKS + 1) * 16)
                    act.wait_ge(adj_used, (b + (MLP0 + r) * BLOCKS) * CHUNKS + (c - 1))
                    for h in range(2):
                        part = slice(h * HALF_QT, (h + 1) * HALF_QT)
                        nc.scalar.activation(adj_hi[(2 * c + h) % PART_BUFS][:, :, :],
                                             ring[:, c, part, :], ACT.Copy).then_inc(hi_ready, 1)
                    if c in ACT_STAGES:
                        before(ACT_STAGES[c])

            act.wait_ge(params_loaded, 48)
            act.wait_ge(bias_ready, 1)
            gru(0)
            with act.Fori(1, BLOCKS) as b:
                gru(b, b - 1)
            lift_functions(BLOCKS - 1)
            small(lift_ask(BLOCKS - 1, 5), ACT.Ln)
            with act.Fori(0, BLOCKS) as b:
                hyper(b)
            for h in range(2):
                exponentials(0, 0, h)
            attn(0)
            with act.Fori(1, BLOCKS - 1) as b:
                attn(b)
            attn(BLOCKS - 1, last=True)
            act.wait_ge(adj_used, MLP0 * BLOCKS * CHUNKS)
            for r in range(ROUNDS):
                if r == 0:
                    round_hi(0, 0, lambda n: small(small_before(ATTN, BLOCKS - 1) + 1, ACT.Sqrt) if n == 1 else None)
                else:
                    round_hi(r, 0, lambda n: mlp(r - 1, BLOCKS - 1, n))
                if r < ROUNDS - 1:
                    with act.Fori(1, BLOCKS) as b:
                        round_hi(r, b, lambda n: mlp(r, b - 1, n))
                else:
                    round_hi(r, 1, lambda n: mlp(r, 0, n))
                    with act.Fori(2, BLOCKS) as b:
                        round_hi(r, b, lambda n: mlp(r, b - 1, n))
            for stage in range(4):
                mlp(ROUNDS - 1, BLOCKS - 1, stage)

        @block.vector
        def _(dve):
            v = nc.vector
            steps = Steps(dve, dve_steps)
            then = steps.then
            row = [sc[:, k, :] for k in range(24)]
            A, B, C, R, Q = row[:5]
            HALF = slice(0, QT)
            REST = slice(QT, 2 * QT)

            def at(buffer, b):
                return buffer[:, bass.ds(b * QT, QT), :]

            def tiles(x):
                return x[:, :].rearrange("p (q f) -> p q f", q=QT)

            def per_row(x):
                return x.unsqueeze(2).to_broadcast([P, QT, F])

            def per_feature(k):
                return brow[:, k, :].unsqueeze(1).to_broadcast([P, QT, F])

            def tt(o, a, b, op):
                return v.tensor_tensor(o, a, b, op)

            def ts(o, a, s1, s2, op0, op1=None):
                return v.tensor_scalar(o, a, s1, s2, op0, *([op1] if op1 is not None else []))

            def stt(o, a, s, b, op0, op1):
                return v.scalar_tensor_tensor(o, a, s, b, op0, op1)

            def ask(n, instruction):
                instruction.then_inc(small_asked, 1)
                dve.wait_ge(small_done, n)

            def layernorm(y, o, n, done):
                for q in range(QT):
                    last = v.bn_stats(stats[:, q, :], y[:, q, :])
                then(last)
                for q in range(QT):
                    last = v.bn_aggr(mv[:, q, :], stats[:, q, :])
                then(last)
                ask(n, ts(s_in[:, HALF], mv[:, :, 1], LN_EPS, None, ALU.add))
                then(v.reciprocal(row[5], s_out[:, HALF]))
                for q in range(QT):
                    last = ts(o[:, q, :], y[:, q, :], mv[:, q, 0:1], row[5][:, q:q + 1],
                              ALU.subtract, ALU.mult)
                done(last)

            def atanh_over(norm, o, n):
                c, u, lg, small, sq, near = row[6:12]
                then(ts(c, norm, MAX_TANH, None, ALU.min))
                ts(u, c, -1.0, 1.0, ALU.mult, ALU.add)
                then(tt(sq, c, c, ALU.mult))
                then(v.reciprocal(u, u))
                ask(n, stt(s_in[:, HALF], c, 1.0, u, ALU.add, ALU.mult))
                then(ts(small, sq, 1 / 9, 1 / 7, ALU.mult, ALU.add))
                for term in (1 / 5, 1 / 3, 1.0):
                    then(tt(small, small, sq, ALU.mult))
                    then(ts(small, small, term, None, ALU.add))
                then(tt(small, small, c, ALU.mult))
                then(ts(lg, s_out[:, HALF], 0.5, None, ALU.mult))
                then(tt(small, small, lg, ALU.subtract))
                then(ts(near, c, 0.125, None, ALU.is_lt))
                then(tt(small, small, near, ALU.mult))
                then(tt(lg, lg, small, ALU.add))
                then(v.reciprocal(u, norm))
                then(tt(o, lg, u, ALU.mult))

            def mobius(root, bias, n):
                nu, th, x2, xy, den = row[12:17]
                then(tt(nu, C, root, ALU.mult))
                then(ts(nu, nu, EPS, None, ALU.max))
                ask(n, v.tensor_copy(s_in[:, HALF], nu))
                then(v.reciprocal(nu, nu))
                then(tt(th, s_out[:, HALF], C, ALU.mult))
                then(tt(th, th, nu, ALU.mult))
                then(tt(x2, th, th, ALU.mult))
                then(tt(x2, x2, Q, ALU.mult))
                then(stt(xy, th, 2.0, R, ALU.mult, ALU.mult))
                then(ts(xy, xy, 1.0, None, ALU.add))
                then(stt(den, x2, bias_sq[:, bias:bias + 1], xy, ALU.mult, ALU.add))
                then(ts(den, den, EPS, None, ALU.max))
                then(v.reciprocal(den, den))
                then(ts(xy, xy, bias_sq[:, bias:bias + 1], None, ALU.add))
                then(tt(xy, xy, th, ALU.mult))
                then(tt(A, xy, den, ALU.mult))
                then(ts(x2, x2, -1.0, 1.0, ALU.mult, ALU.add))
                then(tt(B, x2, den, ALU.mult))

            def moved(y, o, scratch, bias):
                tt(tiles(o), tiles(y), per_row(A), ALU.mult)
                then(tt(tiles(scratch), per_feature(bias), per_row(B), ALU.mult))
                then(tt(o[:, :], o[:, :], scratch[:, :], ALU.add))

            def gru(b):
                feats = xT[:, bass.ds(b * BW, BW)]
                dve.wait_ge(gate_rz, b + 1)
                then(stt(t[1][:, :], e[4][:, :], cols[:, C_HH + 2:C_HH + 3], t[1][:, :],
                         ALU.add, ALU.mult))
                tt(t[1][:, :], t[1][:, :], e[3][:, :], ALU.add).then_inc(gate_lin, 1)
                dve.wait_ge(gate_new, b + 1)
                then(tt(t[1][:, :], feats, t[3][:, :], ALU.subtract))
                then(tt(t[1][:, :], t[1][:, :], t[2][:, :], ALU.mult))
                then(tt(t[1][:, :], t[1][:, :], t[3][:, :], ALU.add))
                tt(t[3][:, :], feats, t[1][:, :], ALU.add).then_inc(dve_part, 1)
                dve.wait_ge(mm_done, mm_before(GRU, b) + 3)
                layernorm(tiles(e[5]), tiles(t[4]), gru_norm_ask(b),
                          lambda i: i.then_inc(ln_out, 1))

            def lift_start(b):
                y, h, s1, s2 = lift
                dve.wait_ge(w_copied, b + 1)
                tt(tiles(s1), at(x_gru, b), at(x_gru, b), ALU.mult)
                tt(s2, y, y, ALU.mult)
                then(tt(tiles(h), tiles(y), per_feature(R_EMBED), ALU.mult))
                v.tensor_reduce(s_in[:, HALF], tiles(s1), AX.X, ALU.add)
                v.tensor_reduce(R, tiles(h), AX.X, ALU.add)
                then(v.tensor_reduce(Q, tiles(s2), AX.X, ALU.add))
                v.tensor_copy(x_sq[:, bass.ds(b * QT, QT)], s_in[:, HALF])
                ask(lift_ask(b, 1), v.tensor_copy(s_in[:, REST], Q))
                norm, root = row[17], row[18]
                ts(norm, s_out[:, HALF], EPS, None, ALU.max)
                then(v.tensor_copy(root, s_out[:, REST]))
                atanh_over(norm, C, lift_ask(b, 2))
                mobius(root, 0, lift_ask(b, 3))
                moved(y, h, s1, R_EMBED)
                then(tt(s1, h, h, ALU.mult))
                ask(lift_ask(b, 4), v.tensor_reduce(s_in[:, HALF], tiles(s1), AX.X, ALU.add))
                then(ts(norm, s_out[:, HALF], EPS, None, ALU.max))

            def lift_end(b):
                atanh_over(row[17], C, lift_ask(b, 5))
                tt(at(lifted, b), tiles(lift[1]), per_row(C), ALU.mult).then_inc(nodes_ready, 1)
                dve.wait_ge(nodes_ready, b + 1)

            def hyper(b):
                dve.wait_ge(mm_done, mm_before(HYPER, b) + 1)
                asked = small_before(HYPER, b)
                qa, na, beta, root = row[17], row[18], row[19], row[20]
                v.tensor_copy(qa, e[1][:, 0:QT])
                ask(asked + 1, v.tensor_copy(s_in[:, HALF], e[1][:, 0:QT]))
                then(ts(na, s_out[:, HALF], EPS, None, ALU.max))
                ask(asked + 2, v.tensor_copy(s_in[:, HALF], na))
                then(v.reciprocal(na, na))
                then(tt(beta, s_out[:, HALF], na, ALU.mult))
                tt(tiles(t[0]), tiles(e[0]), per_row(beta), ALU.mult)
                then(tt(qa, qa, beta, ALU.mult))
                dve.wait_ge(top_copied, b + 1)
                tt(tiles(t[0]), tiles(t[0]), at(top_part, b), ALU.add)
                then(tt(qa, qa, beta, ALU.mult))
                tt(s_in[:, HALF], qa, x_sq[:, bass.ds(b * QT, QT)], ALU.add)
                tt(t[1][:, :], t[0][:, :], t[0][:, :], ALU.mult)
                then(tt(tiles(t[2]), tiles(t[0]), per_feature(R_LAYER), ALU.mult))
                v.tensor_reduce(R, tiles(t[2]), AX.X, ALU.add)
                then(v.tensor_reduce(Q, tiles(t[1]), AX.X, ALU.add))
                ask(asked + 3, v.tensor_copy(s_in[:, REST], Q))
                ts(na, s_out[:, HALF], EPS, None, ALU.max)
                then(v.tensor_copy(root, s_out[:, REST]))
                atanh_over(na, C, asked + 4)
                mobius(root, 1, asked + 5)
                moved(t[0], t[1], t[2], R_LAYER)
                then(tt(tiles(t[1]), tiles(t[1]), at(x_gru, b), ALU.add))
                layernorm(tiles(t[1]), tiles(t[2]), asked + 6, then)
                v.tensor_copy(at(x_hyper, b), tiles(t[2])).then_inc(nodes_ready, 1)
                then(tt(tiles(t[3]), tiles(t[2]), per_feature(R_HV), ALU.mult))
                then(v.tensor_reduce(row[0], tiles(t[3]), AX.X, ALU.add))
                v.tensor_copy(tiles(t[4]), per_row(row[0])).then_inc(dve_part, 1)

            def logits(b, k):
                for h in (1, 0):
                    dve.wait_ge(adj_loaded[2 * k + h], b * 16 + (ATTN * BLOCKS + 1) * 16)
                    half = ring[:, 2 * k + h, :, :].rearrange("p q w -> p (q w)")
                    got = ts(mask[:, h, :], half, 0.0, NEG, ALU.is_equal, ALU.mult)
                    if h:
                        got.then_inc(masked, 1)
                    else:
                        then(got)
                        then(tt(half, half, score_row[:, 0:HALF_ROW], ALU.mult))
                top = row_max[:, b % 2, k:k + 1]
                for h in range(2):
                    half = ring[:, 2 * k + h, :, :].rearrange("p q w -> p (q w)")
                    then(v.tensor_tensor_reduce(
                        out=half, in0=half, in1=mask[:, h, :], scale=1.0, scalar=LOWEST,
                        op0=ALU.add, op1=ALU.max, accum_out=half_max[:, h:h + 1]))
                    if h == 0:
                        dve.wait_ge(scaled, b * QT + (k + 1))
                        then(ts(top, half_max[:, 0:1], 1.0, None, ALU.mult))
                then(ts(top, half_max[:, 1:2], half_max[:, 0:1], None, ALU.max))
                ts(minus_max[:, k:k + 1], row_max[:, b % 2, k:k + 1], -1.0, None,
                   ALU.mult).then_inc(logits_ready, 1)

            def split_value(r, b, x):
                hi, lo = split[r % 2]
                then(v.tensor_copy(at(hi, b), tiles(x)))
                tt(at(lo, b), tiles(x), at(hi, b).bitcast(FP32),
                   ALU.subtract).then_inc(nodes_ready, 1)

            def attn_norm(b):
                dve.wait_ge(adj_used, b * CHUNKS + (ATTN * BLOCKS + 1) * CHUNKS)
                total, neighbours = row[17], row[18]
                then(tt(total, half_sum[:, b % 2, 0, :], half_sum[:, b % 2, 1, :], ALU.add))
                ts(neighbours, row_max[:, b % 2, :], NEG, None, ALU.is_gt)
                then(v.reciprocal(total, total))
                then(tt(total, total, neighbours, ALU.mult))
                then(tt(tiles(t[3]), tiles(acc[:, b % 2, :]), per_row(total), ALU.mult))
                tt(tiles(t[3]), tiles(t[3]), at(x_hyper, b), ALU.add).then_inc(agg_copied, 1)
                dve.wait_ge(agg_copied, b + (ATTN * BLOCKS + 1))
                layernorm(tiles(t[3]), tiles(t[5]), small_before(ATTN, b) + 1, then)
                v.tensor_copy(at(x_attn, b), tiles(t[5]))
                split_value(0, b, t[5])

            def attn(b, before=None):
                for k in range(QT):
                    logits(b, k)
                    if k == 2 and before is not None:
                        attn_norm(before)

            def leaky(o, x):
                return stt(o, x, SLOPE, x, ALU.mult, ALU.max)

            def mlp(r, b, stage):
                p = MLP0 + r
                if stage < 2:
                    dve.wait_ge(hidden_lin, 2 * b + (2 * r * BLOCKS + stage + 1))
                    leaky(t[stage][:, :], t[2 + stage][:, :]).then_inc(dve_part, 1)
                    return
                dve.wait_ge(mm_done, mm_before(p, b) + 3)
                then(tt(tiles(t[4]), tiles(e[2]), per_feature((R_UV, R_VU)[r % 2]), ALU.add))
                then(leaky(t[5][:, :], t[4][:, :]))
                if p < PASSES - 1:
                    split_value(r + 1, b, t[5])
                else:
                    then(tt(tiles(t[5]), tiles(t[5]), at(x_attn, b), ALU.add))
                    layernorm(tiles(t[5]), at(result, b), small_before(p, b) + 1,
                              lambda i: i.then_inc(out_ready, 1))

            def subtract_hi(r, b, before):
                for c in range(CHUNKS):
                    for h in range(2):
                        n = 2 * c + h
                        part = slice(h * HALF_QT, (h + 1) * HALF_QT)
                        dve.wait_ge(hi_ready, (b + r * BLOCKS) * (2 * CHUNKS) + (n + 1))
                        tt(adj_lo[n % PART_BUFS][:, :, :], ring[:, c, part, :],
                           adj_hi[n % PART_BUFS][:, :, :].bitcast(FP32),
                           ALU.subtract).then_inc(lo_ready, 1)
                    if c in DVE_STAGES:
                        before(DVE_STAGES[c])

            dve.wait_ge(params_loaded, 48)
            v.tensor_tensor(bias_rz[:, :], cols[:, C_IH:C_IH + 2], cols[:, C_HH:C_HH + 2], ALU.add)
            v.memset(s_in[:, :], 1.0)
            for k, r in enumerate((R_EMBED, R_LAYER)):
                then(tt(t[k][:, 0:F], brow[:, r, :], brow[:, r, :], ALU.mult))
                last = v.tensor_reduce(bias_sq[:, k:k + 1], t[k][:, 0:F], AX.X, ALU.add)
            last.then_inc(bias_ready, 1)
            dve.wait_ge(bias_ready, 1)
            dve.wait_ge(feats_loaded, 16)
            steps.restart()
            gru(0)
            with dve.Fori(1, BLOCKS) as b:
                steps.restart()
                lift_start(b - 1)
                gru(b)
                lift_end(b - 1)
            steps.restart()
            lift_start(BLOCKS - 1)
            lift_end(BLOCKS - 1)
            with dve.Fori(0, BLOCKS) as b:
                steps.restart()
                hyper(b)
            dve.wait_ge(score_ready, BLOCKS)
            steps.restart()
            attn(0)
            with dve.Fori(1, BLOCKS) as b:
                steps.restart()
                attn(b, b - 1)
            for r in range(ROUNDS):
                steps.restart()
                if r == 0:
                    subtract_hi(0, 0, lambda n: attn_norm(BLOCKS - 1) if n == 0 else None)
                else:
                    subtract_hi(r, 0, lambda n: mlp(r - 1, BLOCKS - 1, n))
                with dve.Fori(1, BLOCKS) as b:
                    steps.restart()
                    subtract_hi(r, b, lambda n: mlp(r, b - 1, n))
            steps.restart()
            for stage in range(3):
                mlp(ROUNDS - 1, BLOCKS - 1, stage)


def kernel(x, adj, L0_gnn_W_msg, L0_gnn_b_msg, L0_gnn_W_ih, L0_gnn_W_hh, L0_gnn_b_ih, L0_gnn_b_hh,
           L1_gnn_embed, L1_gnn_layer, L1_gnn_embed_bias, L1_gnn_layer_bias, L2_gnn_H_v,
           L3_gnn_v_node_feats, L3_gnn_uv_W1, L3_gnn_uv_b1, L3_gnn_uv_W2, L3_gnn_uv_b2,
           L3_gnn_uv_W3, L3_gnn_uv_b3, L3_gnn_vu_W1, L3_gnn_vu_b1, L3_gnn_vu_W2, L3_gnn_vu_b2,
           L3_gnn_vu_W3, L3_gnn_vu_b3):
    import numpy as np
    import concourse.bacc as bacc
    from concourse.bass_utils import run_bass_kernel_spmd

    def a(v):
        return np.asarray(v)

    adj_blocks = a(adj).reshape(BLOCKS, BW, CHUNKS, QT, P).transpose(0, 2, 4, 3, 1)
    adj_rows = a(adj).reshape(BLOCKS, QT, P, 2, HALF_ROW)
    xs = a(x)
    weights = np.concatenate(
        [a(L0_gnn_W_msg).T, a(L0_gnn_W_ih).T, a(L0_gnn_W_hh).T, a(L1_gnn_embed),
         a(L1_gnn_layer)[:F], a(L1_gnn_layer)[F:], a(L3_gnn_uv_W1), a(L3_gnn_uv_W2),
         a(L3_gnn_uv_W3), a(L3_gnn_vu_W1), a(L3_gnn_vu_W2), a(L3_gnn_vu_W3)], axis=1)
    columns = np.stack(
        [a(L0_gnn_b_msg), *a(L0_gnn_b_ih).reshape(3, F), *a(L0_gnn_b_hh).reshape(3, F),
         a(L3_gnn_uv_b1), a(L3_gnn_uv_b2), a(L3_gnn_vu_b1), a(L3_gnn_vu_b2)], axis=1)
    rows = np.concatenate([a(L1_gnn_embed_bias), a(L1_gnn_layer_bias), a(L2_gnn_H_v)[:, 0],
                           a(L3_gnn_uv_b3), a(L3_gnn_vu_b3)])[None, :]
    arrays = {
        "adj": adj_blocks, "adj_rows": adj_rows, "x_nodes": xs.reshape(TILES, P, F).transpose(1, 0, 2),
        "x_feats": xs.T, "weights": weights.reshape(F, W_ALL, P), "columns": columns, "rows": rows,
    }
    arrays = {f"in_{k}": np.ascontiguousarray(v) for k, v in arrays.items()}
    nc = bacc.Bacc("TRN2", target_bir_lowering=False, num_devices=1)
    args = [nc.dram_tensor(k, v.shape, FP32, kind="ExternalInput").ap() for k, v in arrays.items()]
    args.append(nc.dram_tensor("out", (P, TILES, F), FP32, kind="ExternalOutput").ap())
    build(nc, *args)
    r = run_bass_kernel_spmd(nc, [arrays], core_ids=[0])
    return np.ascontiguousarray(np.asarray(r.results[0]["out"]).transpose(1, 0, 2)).reshape(N, F)
```

```python
import concourse.bass as bass
from concourse import mybir
from contextlib import ExitStack

FP32 = mybir.dt.float32
FP32R = mybir.dt.float32r
ALU = mybir.AluOpType
ACT = mybir.ActivationFunctionType
AX = mybir.AxisListType

N, F = 4096, 128
P = 128
TILES = N // P
BW = 512
BLOCKS = N // BW
QT = BW // P
CHUNKS = TILES // QT
NEG = -1e9
EPS = 1e-7
MAX_TANH = 1.0 - 1e-6
LN_EPS = 1e-5
SLOPE = 0.01

GRU, HYPER, ATTN, MLP0, ROUNDS = 0, 1, 2, 3, 5
PASSES = MLP0 + ROUNDS
SMALL = {GRU: 5, HYPER: 6, ATTN: 1}
GROUPS, TURN_BUFS, TURN_LEAD = TILES // QT, 4, 2
HALF_ROW = N // 2
LOWEST = -3.0e38
ATTN_ASK, ATTN_END, ATTN_SQRT = 2, 3, (1, 1)
HALVES = 2 * CHUNKS
HALF_QT, HI_BUFS, GRU_HI_BUFS = QT // 2, 8, 4
WHOLE_CHUNKS = {GRU: (0, 1, 2, 5), HYPER: (0, 1, 7)}
GRU_SPLIT_AT = ((3,), (4,), (6,), (7,))
GRU_LO_AT = ((3,), (4,), (6,), (7,))
POOL_HALVES = {GRU: (7, 9, 13, 15), HYPER: (4, 5, 7, 9, 11, 12, 13), MLP0: (3, 7, 11, 15)}
TAIL_ASK, TAIL_SQRT, TAIL_END, TAIL_POOL = 1, 2, 2, 7
SCORE_SLOT = 4
ACT_STAGES, DVE_STAGES = {1: 0, 3: 1, 5: 2, 7: 3}, {3: 0, 5: 1, 7: 2}

(W_MSG, W_IH, W_HH, W_EMBED, W_TOP, W_BOT, W_UV, W_VU, W_ALL) = (0, 1, 4, 7, 8, 9, 10, 13, 16)
(C_MSG, C_IH, C_HH, C_UV, C_VU, C_ALL) = (0, 1, 4, 7, 9, 11)
R_EMBED, R_LAYER, R_HV, R_UV, R_VU, R_ALL = range(6)


class Steps:

    def __init__(self, engine, sem):
        self.engine, self.sem, self.n = engine, sem, 0

    def count(self, instruction):
        self.n += 1
        instruction.then_inc(self.sem, 1)

    def wait(self):
        self.engine.wait_ge(self.sem, self.n)

    def then(self, instruction):
        self.count(instruction)
        self.wait()

    def restart(self):
        self.engine.sem_clear(self.sem)
        self.n = 0


def small_before(layer, b):
    gru = SMALL[GRU] * BLOCKS + 1
    hyper = gru + SMALL[HYPER] * BLOCKS
    at = {HYPER: gru, ATTN: hyper, PASSES - 1: hyper + SMALL[ATTN] * BLOCKS}[layer]
    return b * SMALL.get(layer, 1) + at


def pool_halves(p):
    return POOL_HALVES[min(p, MLP0)]


def whole(p, c):
    return c in WHOLE_CHUNKS.get(p, ())


def split_chunks(p):
    return [c for c in range(CHUNKS) if not whole(p, c)]


def hi_buffer(p, c, h):
    if p == GRU:
        return (2 * split_chunks(GRU).index(c) + h) % GRU_HI_BUFS
    return (2 * c + h) % HI_BUFS


def split_count(p, b, n, by=None):
    def of(q):
        return [h for h in range(HALVES) if not whole(q, h // 2)
                and by in (None, "pool" if h in pool_halves(q) else "vector")]

    before = -len(of(GRU))
    if p > GRU:
        before += BLOCKS * len(of(GRU)) - len(of(HYPER))
    if p > HYPER:
        before += BLOCKS * len(of(HYPER)) + (p - MLP0) * BLOCKS * len(of(MLP0))
    return b * len(of(p)) + (before + sum(h <= n for h in of(p)))


def in_pass(b):
    return not isinstance(b, int) or 0 <= b < BLOCKS


HYPER_EARLY = {4: (1, ACT.Sqrt), 5: (2, ACT.Tanh), 6: (3, ACT.Sqrt), 7: (4, ACT.Ln)}
HYPER_LATE = {0: (5, ACT.Tanh), 2: (6, ACT.Sqrt)}


def lift_ask(b, k):
    return b * SMALL[GRU] + (1 + k)


def gru_norm_ask(b):
    return 1 if isinstance(b, int) and b == 0 else b * SMALL[GRU]


def build(nc, adj, adj_rows, x_nodes, x_feats, weights, columns, rows, out):
    with ExitStack() as ctx:
        def sb(name, *shape):
            return ctx.enter_context(nc.sbuf_tensor(name, [P, *shape], FP32))

        def sem(name):
            return ctx.enter_context(nc.semaphore(name))

        def sb_at(name, *shape):
            tensor = sb(name, *shape)
            size = 4
            for n in shape:
                size *= n
            return tensor, nc.sbuf_base - size

        ring, ring_at = sb_at("ring", CHUNKS, QT, BW)
        x_in, x_in_at = sb_at("x_in", TILES, F)
        x_gru, x_gru_at = sb_at("x_gru", TILES, F)
        x_hyper = x_gru
        lifted, lifted_at = sb_at("lifted", TILES, F)
        x_attn = lifted
        top_part, top_part_at = sb_at("top_part", TILES, F)
        xT, xT_at = sb_at("xT", N)
        work, work_at = sb_at("work", 4, HALF_ROW)
        def over(name, offset, *shape):
            return nc.alloc_sbuf_tensor_at(name, [P, *shape], FP32R, offset=offset)

        hyper_hi = over("hyper_hi", x_in_at, TILES, F)
        hyper_lo = over("hyper_lo", lifted_at, TILES, F)
        split = [(over("value_hi0", x_in_at, TILES, F), over("value_lo0", top_part_at, TILES, F)),
                 (over("value_hi1", x_gru_at, TILES, F), over("value_lo1", xT_at, TILES, F))]
        adj_lo = over("adj_lo", ring_at, CHUNKS, QT, BW)
        adj_hi = [over(f"adj_hi{i}", work_at + i * 4 * HALF_QT * BW, HALF_QT, BW)
                  for i in range(HI_BUFS)]
        lift = [work[:, 2, i * BW:(i + 1) * BW] for i in range(4)]
        x_hi = over("x_hi", work_at + 3 * 4 * HALF_ROW, len(split_chunks(GRU)), QT, F)
        x_lo = over("x_lo", x_in_at, TILES, F)
        result = x_gru
        w = sb("w", W_ALL, P)
        cols = sb("cols", C_ALL)
        bias_rz = sb("bias_rz", 2)
        brow = sb("brow", R_ALL, F)
        ident = sb("ident", P)
        ones = sb("ones", P)
        x_sq = sb("x_sq", TILES)
        bias_sq = sb("bias_sq", 2)
        aggT = sb("aggT", BW)
        sqT = sb("sqT", BW)
        t = [sb(f"t{i}", BW) for i in range(6)]
        score_row = xT
        mask = work[:, 0:2, :]
        turned = [work[:, 2 + i // QT, (i % QT) * BW:(i % QT + 1) * BW] for i in range(TURN_BUFS)]
        half_max = sb("half_max", 2)
        absorbed = sb("absorbed", 1)
        minus_max = sb("minus_max", 2, QT)
        half_sum = sb("half_sum", 2, 2, QT)
        stats = sb("stats", QT, 6)
        mv = sb("mv", QT, 2)
        s_in = sb("s_in", 2 * QT)
        s_out = sb("s_out", 2 * QT)
        sc = sb("sc", 24, QT)

        acc = ctx.enter_context(nc.psum_tensor("acc", [P, 2, BW], FP32))
        epi = ctx.enter_context(nc.psum_tensor("epi", [P, 6, BW], FP32))
        e = [epi[:, i, :] for i in range(6)]

        adj_loaded = [sem(f"adj_loaded{c}") for c in range(CHUNKS)]
        adj_used = sem("adj_used")
        params_loaded = sem("params_loaded")
        first_nodes_loaded, nodes_loaded = sem("first_nodes_loaded"), sem("nodes_loaded")
        feats_loaded = sem("feats_loaded")
        consts_ready = sem("consts_ready")
        bias_ready = sem("bias_ready")
        agg_copied = sem("agg_copied")
        mm_done = sem("mm_done")
        act_part = sem("act_part")
        dve_part = sem("dve_part")
        gate_lin = sem("gate_lin")
        gate_new = sem("gate_new")
        gate_rz = sem("gate_rz")
        ln_out = sem("ln_out")
        w_copied = sem("w_copied")
        top_copied = sem("top_copied")
        small_asked, small_done = sem("small_asked"), sem("small_done")
        nodes_ready = sem("nodes_ready")
        hidden_lin = sem("hidden_lin")
        score_ready = sem("score_ready")
        masked = sem("masked")
        scaled = sem("scaled")
        logits_ready = sem("logits_ready")
        probs_ready = sem("probs_ready")
        probs_turned = sem("probs_turned")
        turn_copied = sem("turn_copied")
        hi_ready = sem("hi_ready")
        lo_ready = sem("lo_ready")
        pool_lo_ready = sem("pool_lo_ready")
        x_hi_ready = sem("x_hi_ready")
        x_lo_ready = sem("x_lo_ready")
        value_hi_ready = sem("value_hi_ready")
        value_lo_ready = sem("value_lo_ready")
        norm_ready = sem("norm_ready")
        score_made = sem("score_made")
        score_turned = sem("score_turned")
        out_ready, out_stored = sem("out_ready"), sem("out_stored")
        dve_steps, pool_steps = sem("dve_steps"), sem("pool_steps")

        SLOTS = {GRU: 5, HYPER: 1, ATTN: 0}

        def mm_before(p, b):
            per = [SLOTS.get(k, 3) for k in range(PASSES)]
            return b * per[p] + sum(per[:p]) * BLOCKS

        block = ctx.enter_context(nc.Block())

        @block.sync
        def _(sp):
            def load(g, b, c, first=False):
                if not first:
                    sp.wait_ge(adj_used, (g - 1) * CHUNKS + c + 1)
                sp.dma_start(ring[:, c, :, :], adj[b, c]).then_inc(adj_loaded[c], 16)

            def load_rows(g, b, c):
                sp.wait_ge(adj_used, (g - 1) * CHUNKS + c + 1)
                sp.dma_start(ring[:, c, :, :].rearrange("p q w -> p (q w)"),
                             adj_rows[b, c // 2, :, c % 2, :]).then_inc(adj_loaded[c], 16)

            sp.dma_start(x_in[:, 0:QT, :], x_nodes[:, 0:QT, :]).then_inc(first_nodes_loaded, 16)
            for c in range(CHUNKS):
                load(0, 0, c, first=True)
                if c == 0:
                    sp.dma_start(x_in[:, QT:, :], x_nodes[:, QT:, :]).then_inc(nodes_loaded, 16)
                if c == 1:
                    sp.dma_start(w[:, :, :], weights).then_inc(params_loaded, 16)
                    sp.dma_start(cols[:, :], columns).then_inc(params_loaded, 16)
                    sp.dma_start(brow[:, :, :].rearrange("p r f -> p (r f)"),
                                 rows.to_broadcast([P, R_ALL * F])).then_inc(params_loaded, 16)
            sp.dma_start(xT[:, :], x_feats).then_inc(feats_loaded, 16)
            for p in range(PASSES - 1):
                with sp.Fori(0 if p else 1, BLOCKS) as b:
                    for c in range(CHUNKS):
                        (load_rows if p == ATTN else load)(b + p * BLOCKS, b, c)

            def last_round(b):
                for c in range(CHUNKS):
                    load(b + (PASSES - 1) * BLOCKS, b, c)

            def store(b):
                sp.wait_ge(out_ready, b + 1)
                sp.dma_start(out[:, bass.ds(b * QT, QT), :],
                             result[:, bass.ds(b * QT, QT), :]).then_inc(out_stored, 16)

            last_round(0)
            last_round(1)
            with sp.Fori(2, BLOCKS) as b:
                last_round(b)
                store(b - 2)
            store(BLOCKS - 2)
            store(BLOCKS - 1)
            sp.wait_ge(out_stored, 16 * BLOCKS)

        @block.gpsimd
        def _(pool):
            steps = Steps(pool, pool_steps)
            steps.then(nc.gpsimd.memset(ident[:, :], 0.0))
            nc.gpsimd.affine_select(out=ident[:, :], in_=ident[:, :], compare_op=ALU.not_equal,
                                    fill=1.0, base=0, pattern=[[-1, P]],
                                    channel_multiplier=1).then_inc(consts_ready, 1)
            nc.gpsimd.memset(ones[:, :], 1.0).then_inc(consts_ready, 1)

            def subtract(p, b):
                for n in pool_halves(p):
                    c, h = n // 2, n % 2
                    if whole(p, c):
                        continue
                    part = slice(h * HALF_QT, (h + 1) * HALF_QT)
                    pool.wait_ge(hi_ready, split_count(p, b, n))
                    nc.gpsimd.tensor_tensor(adj_lo[:, c, part, :], ring[:, c, part, :],
                                            adj_hi[hi_buffer(p, c, h)][:, :, :].bitcast(FP32),
                                            ALU.subtract).then_inc(pool_lo_ready, 1)
                    if n == TAIL_POOL and p == MLP0 and isinstance(b, int):
                        attn_end(BLOCKS - 1)

            def attn_end(b):
                pool.wait_ge(norm_ready, b + 1)
                x = x_attn[:, bass.ds(b * QT, QT), :]
                hi, lo = (part[:, bass.ds(b * QT, QT), :] for part in split[0])
                steps.then(nc.gpsimd.tensor_copy(hi, x))
                nc.gpsimd.tensor_tensor(lo, x, hi.bitcast(FP32),
                                        ALU.subtract).then_inc(nodes_ready, 1)

            for p in (GRU, HYPER):
                with pool.Fori(1, BLOCKS) as b:
                    subtract(p, b)
            pool.wait_ge(score_ready, BLOCKS)
            def scale(b):
                for k in range(QT):
                    pool.wait_ge(masked, b * QT + (k + 1))
                    half = ring[:, 2 * k + 1, :, :].rearrange("p q w -> p (q w)")
                    nc.gpsimd.tensor_tensor(half, half, score_row[:, HALF_ROW:],
                                            ALU.mult).then_inc(scaled, 1)

            scale(0)
            with pool.Fori(1, BLOCKS) as b:
                steps.restart()
                scale(b)
                attn_end(b - 1)
            steps.restart()

            subtract(MLP0, 0)
            with pool.Fori(1, BLOCKS) as b:
                subtract(MLP0, b)
            for p in range(MLP0 + 1, PASSES):
                with pool.Fori(0, BLOCKS) as b:
                    subtract(p, b)

        @block.tensor
        def _(pe):
            def mm(o, lhsT, rhs, start=True, stop=True):
                return nc.tensor.matmul(o, lhsT, rhs, start=start, stop=stop)

            def weight(k):
                return w[:, k, :]

            def gru_msg(b):
                pe.wait_ge(agg_copied, b + 1)
                mm(e[0][:, :], weight(W_MSG), aggT[:, :]).then_inc(mm_done, 1)

            def gru_gates(b):
                pe.wait_ge(act_part, b * 2 + 1)
                feats = xT[:, bass.ds(b * BW, BW)]
                for g in range(2):
                    mm(e[1 + g][:, :], weight(W_IH + g), t[0][:, :], stop=False)
                    mm(e[1 + g][:, :], weight(W_HH + g), feats, start=False)
                mm(e[3][:, :], weight(W_IH + 2), t[0][:, :])
                mm(e[4][:, :], weight(W_HH + 2), feats).then_inc(mm_done, 1)

            def to_nodes(dst, src, done):
                for q in range(QT):
                    last = nc.tensor.transpose(dst[:, q * P:(q + 1) * P],
                                               src[:, q * P:(q + 1) * P], ident[:, :])
                last.then_inc(done, 1)

            def gru_turn(b):
                pe.wait_ge(dve_part, b + 1)
                to_nodes(e[5], t[3], mm_done)

            def gru_turn_back(b):
                pe.wait_ge(ln_out, b + 1)
                to_nodes(e[0], t[4], mm_done)

            def gru_embed(b):
                pe.wait_ge(act_part, b * 2 + 2)
                for k, o in ((W_EMBED, e[1]), (W_TOP, e[2])):
                    for q in range(QT):
                        s = slice(q * P, (q + 1) * P)
                        last = mm(o[:, s], t[5][:, s], weight(k))
                last.then_inc(mm_done, 1)

            def hyper_out(b):
                pe.wait_ge(agg_copied, b + (BLOCKS + 1))
                for q in range(QT):
                    s = slice(q * P, (q + 1) * P)
                    mm(e[0][:, s], aggT[:, s], weight(W_BOT))
                for q in range(QT):
                    last = mm(e[1][:, q:q + 1], sqT[:, q * P:(q + 1) * P], ones[:, 0:1])
                last.then_inc(mm_done, 1)

            def hyper_score(b):
                pe.wait_ge(score_made, b + 1)
                to_nodes(e[2], t[4], score_turned)

            def mlp_slots(r):
                k = (W_UV, W_VU)[r % 2]
                n = r * BLOCKS

                def first(b):
                    pe.wait_ge(agg_copied, b + (MLP0 * BLOCKS + n + 1))
                    mm(e[0][:, :], weight(k), aggT[:, :]).then_inc(mm_done, 1)

                def second(b):
                    pe.wait_ge(dve_part, 2 * b + (BLOCKS + 2 * n + 1))
                    mm(e[1][:, :], weight(k + 1), t[0][:, :]).then_inc(mm_done, 1)

                def third(b):
                    pe.wait_ge(dve_part, 2 * b + (BLOCKS + 2 * n + 2))
                    for q in range(QT):
                        s = slice(q * P, (q + 1) * P)
                        last = mm(e[2][:, s], t[1][:, s], weight(k + 2))
                    last.then_inc(mm_done, 1)

                return {0: first, 2: second, 4: third}

            slots = [{0: gru_msg, 1: gru_gates, 4: gru_turn, 6: gru_turn_back, 7: gru_embed},
                     {1: hyper_out}, {}]
            slots += [mlp_slots(r) for r in range(ROUNDS)]

            gru_tail = {0: gru_msg, 1: gru_gates, 2: gru_turn, 4: gru_turn_back, 5: gru_embed}

            def run_slot(p, b, c):
                at = gru_tail if p == GRU and isinstance(b, int) and b == BLOCKS - 1 else slots[p]
                if c in at:
                    at[c](b)

            def run_slots(p, b, c):
                if not isinstance(b, int) or b > 0:
                    run_slot(p, b - 1, c)
                elif p:
                    run_slot(p - 1, BLOCKS - 1, c)
                if p == HYPER and c == SCORE_SLOT and (not isinstance(b, int) or b > 1):
                    hyper_score(b - 2)

            def aggregate_chunk(p, value, b, bank, c):
                pe.wait_ge(adj_loaded[c], (b + p * BLOCKS) * 16 + 16)
                for q in range(QT):
                    j = c * QT + q
                    last = mm(acc[:, bank, :], value[:, j, :], ring[:, c, q, :],
                              start=j == 0, stop=j == TILES - 1)
                last.then_inc(adj_used, 1)
                run_slots(p, b, c)

            def aggregate(p, value, b, bank):
                for c in range(CHUNKS):
                    if isinstance(b, int) and b == 0:
                        if p:
                            pe.wait_ge(nodes_ready, (p - 1) * BLOCKS + c + 1)
                        elif c < 2:
                            pe.wait_ge((first_nodes_loaded, nodes_loaded)[c], 16)
                    aggregate_chunk(p, value, b, bank, c)

            def aggregate_split(p, b, bank):
                def value_parts(c, j):
                    if p == GRU:
                        return x_hi[:, split_chunks(GRU).index(c), j - c * QT, :], x_lo[:, j, :]
                    hi, lo = (hyper_hi, hyper_lo) if p == HYPER else split[(p - MLP0) % 2]
                    return hi[:, j, :], lo[:, j, :]

                for c in range(CHUNKS):
                    if p > HYPER and isinstance(b, int) and b == 0:
                        pe.wait_ge(nodes_ready, (p - 1) * BLOCKS + c + 1)
                    if whole(p, c):
                        aggregate_chunk(p, (x_in, lifted)[p], b, bank, c)
                        continue
                    for h in range(2):
                        n = 2 * c + h
                        if n in pool_halves(p):
                            pe.wait_ge(pool_lo_ready, split_count(p, b, n, "pool"))
                        else:
                            pe.wait_ge(lo_ready, split_count(p, b, n, "vector"))
                        for q in range(HALF_QT):
                            j = c * QT + h * HALF_QT + q
                            part_hi = adj_hi[hi_buffer(p, c, h)][:, q, :]
                            part_lo = adj_lo[:, c, h * HALF_QT + q, :]
                            value_hi, value_lo = value_parts(c, j)
                            mm(acc[:, bank, :], value_hi, part_hi, start=j == 0, stop=False)
                            mm(acc[:, bank, :], value_hi, part_lo, start=False, stop=False)
                            last = mm(acc[:, bank, :], value_lo, part_hi,
                                      start=False, stop=j == TILES - 1)
                    last.then_inc(adj_used, 1)
                    run_slots(p, b, c)

            def attend(b, bank):
                def turn(k, g):
                    n = k * GROUPS + g
                    if g % (GROUPS // 2) == 0:
                        pe.wait_ge(probs_ready, b * (2 * QT) + (2 * k + 2 * g // GROUPS + 1))
                    if not (first and n < TURN_BUFS):
                        pe.wait_ge(turn_copied, b * (QT * GROUPS) + (n - TURN_BUFS + 1))
                    row = ring[:, 2 * k:2 * k + 2, :, :].rearrange("p c q w -> p (c q w)")
                    for q in range(QT):
                        j = g * QT + q
                        last = nc.tensor.transpose(e[g % TURN_BUFS][:, q * P:(q + 1) * P],
                                                   row[:, j * P:(j + 1) * P], ident[:, :])
                    last.then_inc(probs_turned, 1)

                def aggregate_group(k, g):
                    n = k * GROUPS + g
                    pe.wait_ge(turn_copied, b * (QT * GROUPS) + (n + 1))
                    for q in range(QT):
                        j = g * QT + q
                        last = mm(acc[:, bank, k * P:(k + 1) * P],
                                  turned[g % TURN_BUFS][:, q * P:(q + 1) * P],
                                  x_hyper[:, j, :], start=j == 0, stop=j == TILES - 1)
                    if g % (GROUPS // 2) == GROUPS // 2 - 1:
                        last.then_inc(adj_used, 1)

                first = isinstance(b, int) and b == 0
                every = [(k, g) for k in range(QT) for g in range(GROUPS)]
                for n in range(len(every) + TURN_LEAD):
                    if n < len(every):
                        turn(*every[n])
                    if n >= TURN_LEAD:
                        aggregate_group(*every[n - TURN_LEAD])

            for p in range(PASSES):

                if p == ATTN:
                    hyper_out(BLOCKS - 1)
                    hyper_score(BLOCKS - 2)
                    hyper_score(BLOCKS - 1)
                    attend(0, 0)
                    with pe.Fori(0, (BLOCKS - 2) // 2) as i:
                        for k in (1, 2):
                            attend(i * 2 + k, k % 2)
                    attend(BLOCKS - 1, (BLOCKS - 1) % 2)
                    continue

                def one(b, bank):
                    if p < ATTN and isinstance(b, int) and b == 0:
                        aggregate(p, (x_in, lifted)[p], b, bank)
                    else:
                        aggregate_split(p, b, bank)

                one(0, 0)
                if p == GRU:
                    pe.wait_ge(params_loaded, 48)
                    pe.wait_ge(consts_ready, 2)
                    pe.wait_ge(feats_loaded, 16)
                    pe.wait_ge(x_hi_ready, len(split_chunks(GRU)))
                    pe.wait_ge(x_lo_ready, len(split_chunks(GRU)))
                if p == HYPER:
                    pe.wait_ge(value_hi_ready, len(split_chunks(HYPER)))
                    pe.wait_ge(value_lo_ready, len(split_chunks(HYPER)))
                    one(1, 1)
                    one(2, 0)
                with pe.Fori(1 if p == HYPER else 0, (BLOCKS - 2) // 2) as i:
                    for k in (1, 2):
                        one(i * 2 + k, k % 2)
                one(BLOCKS - 1, (BLOCKS - 1) % 2)
            for c in range(CHUNKS):
                run_slot(PASSES - 1, BLOCKS - 1, c)

        @block.scalar
        def _(act):
            def aggregated(p, b):
                act.wait_ge(adj_used, (b + p * BLOCKS) * CHUNKS + CHUNKS)

            def temps_free(p, b):
                if p < PASSES - 1:
                    act.wait_ge(nodes_ready, b + p * BLOCKS)
                elif not isinstance(b, int):
                    act.wait_ge(out_ready, b)

            def small(n, func):
                act.wait_ge(small_asked, n)
                nc.scalar.activation(s_out[:, :], s_in[:, :], func).then_inc(small_done, 1)

            def gru(b, lifting=None, splitting=True):
                def round_at(place):
                    for c in GRU_SPLIT_AT[place] if splitting else ():
                        round_chunk(GRU, b + 1, c)

                aggregated(GRU, b)
                nc.scalar.activation(aggT[:, :], acc[:, b % 2, :], ACT.Copy).then_inc(agg_copied, 1)
                lift_small(lifting, 1, ACT.Sqrt)
                act.wait_ge(mm_done, mm_before(GRU, b) + 1)
                nc.scalar.activation(t[0][:, :], e[0][:, :], ACT.Relu,
                                     bias=cols[:, C_MSG:C_MSG + 1]).then_inc(act_part, 1)
                round_at(0)
                lift_small(lifting, 2, ACT.Ln)
                round_at(1)
                lift_small(lifting, 3, ACT.Tanh)
                act.wait_ge(mm_done, mm_before(GRU, b) + 2)
                for g in range(2):
                    last = nc.scalar.activation(t[1 + g][:, :], e[1 + g][:, :], ACT.Sigmoid,
                                                bias=bias_rz[:, g:g + 1])
                last.then_inc(gate_rz, 1)
                act.wait_ge(gate_lin, b + 1)
                nc.scalar.activation(t[3][:, :], t[1][:, :], ACT.Tanh,
                                     bias=cols[:, C_IH + 2:C_IH + 3]).then_inc(gate_new, 1)
                round_at(2)
                round_at(3)
                small(gru_norm_ask(b), ACT.Sqrt)
                act.wait_ge(ln_out, b + 1)
                nc.scalar.activation(x_gru[:, bass.ds(b * QT, QT), :].rearrange("p q f -> p (q f)"),
                                     t[4][:, :], ACT.Copy)
                lift_small(lifting, 5, ACT.Ln)
                act.wait_ge(mm_done, mm_before(GRU, b) + 4)
                nc.scalar.activation(t[5][:, :], e[0][:, :], ACT.Copy).then_inc(act_part, 1)
                act.wait_ge(mm_done, mm_before(GRU, b) + 5)
                nc.scalar.activation(lift[0], e[1][:, :], ACT.Copy).then_inc(w_copied, 1)
                top = top_part[:, bass.ds(b * QT, QT), :].rearrange("p q f -> p (q f)")
                nc.scalar.activation(top, e[2][:, :], ACT.Copy).then_inc(top_copied, 1)

            def lift_small(b, k, func):
                if b is not None:
                    small(lift_ask(b, k), func)

            def hyper(b, c):
                if c == 2 and in_pass(b - 1):
                    aggregated(HYPER, b - 1)
                    nc.scalar.activation(aggT[:, :], acc[:, (b - 1) % 2, :], ACT.Copy)
                    nc.scalar.activation(sqT[:, :], acc[:, (b - 1) % 2, :],
                                         ACT.Square).then_inc(agg_copied, 1)
                if c in HYPER_LATE and in_pass(b - 2):
                    n, func = HYPER_LATE[c]
                    small(small_before(HYPER, b - 2) + n, func)
                if c in HYPER_EARLY and in_pass(b - 1):
                    n, func = HYPER_EARLY[c]
                    small(small_before(HYPER, b - 1) + n, func)
                if c == 5 and in_pass(b - 2):
                    act.wait_ge(score_turned, b - 1)
                    nc.scalar.activation(score_row[:, bass.ds((b - 2) * BW, BW)], e[2][:, :],
                                         ACT.Copy).then_inc(score_ready, 1)

            def exponentials(b, k, h):
                b, k = (b + 1, 0) if k == QT else (b, k)
                act.wait_ge(logits_ready, b * QT + (k + 1))
                half = ring[:, 2 * k + h, :, :].rearrange("p q w -> p (q w)")
                nc.scalar.activation(half, half, ACT.Exp, bias=minus_max[:, b % 2, k:k + 1],
                                     accum_out=half_sum[:, b % 2, h, k:k + 1])\
                    .then_inc(probs_ready, 1)

            def attn(b, last=False):
                for k in range(QT):
                    for g in range(GROUPS):
                        act.wait_ge(probs_turned, (b * QT + k) * GROUPS + (g + 1))
                        nc.scalar.activation(turned[g % TURN_BUFS][:, :], e[g % TURN_BUFS][:, :],
                                             ACT.Copy).then_inc(turn_copied, 1)
                        if g in (1, 5) and not (last and k == QT - 1):
                            exponentials(b, k + 1, g // (GROUPS // 2))
                        if (k, g) == ATTN_SQRT and not (isinstance(b, int) and b == 0):
                            small(small_before(ATTN, b - 1) + 1, ACT.Sqrt)

            def mlp(r, b, stage):
                p = MLP0 + r
                if stage == 0:
                    aggregated(p, b)
                    nc.scalar.activation(aggT[:, :], acc[:, b % 2, :],
                                         ACT.Copy).then_inc(agg_copied, 1)
                    temps_free(p, b)
                elif stage < 3:
                    k = stage - 1
                    act.wait_ge(mm_done, mm_before(p, b) + (k + 1))
                    c = (C_UV, C_VU)[r % 2] + k
                    nc.scalar.activation(t[2 + k][:, :], e[k][:, :], ACT.Identity,
                                         bias=cols[:, c:c + 1]).then_inc(hidden_lin, 1)
                elif p == PASSES - 1:
                    small(small_before(p, b) + 1, ACT.Sqrt)

            def round_chunk(p, b, c):
                act.wait_ge(adj_loaded[c], b * 16 + (p * BLOCKS + 1) * 16)
                if p == GRU:
                    m = split_chunks(GRU).index(c) - GRU_HI_BUFS // 2
                    used = split_chunks(GRU)[m] - (CHUNKS if m < 0 else 0)
                else:
                    used = c - HI_BUFS // 2
                act.wait_ge(adj_used, (b + p * BLOCKS) * CHUNKS + (used + 1))
                for h in range(2):
                    part = slice(h * HALF_QT, (h + 1) * HALF_QT)
                    nc.scalar.activation(adj_hi[hi_buffer(p, c, h)][:, :, :],
                                         ring[:, c, part, :], ACT.Copy).then_inc(hi_ready, 1)

            def round_hi(p, b, after):
                for c in range(CHUNKS):
                    if not whole(p, c):
                        round_chunk(p, b, c)
                    after(c)

            def stages(r, b):
                return lambda c: mlp(r, b, ACT_STAGES[c]) if c in ACT_STAGES else None

            act.wait_ge(nodes_loaded, 16)
            for m, c in enumerate(split_chunks(GRU)):
                nc.scalar.activation(x_hi[:, m, :, :], x_in[:, c * QT:(c + 1) * QT, :],
                                     ACT.Copy).then_inc(x_hi_ready, 1)
            act.wait_ge(params_loaded, 48)
            act.wait_ge(bias_ready, 1)
            gru(0)
            with act.Fori(1, BLOCKS - 1) as b:
                gru(b, b - 1)
            gru(BLOCKS - 1, BLOCKS - 2, splitting=False)
            for k, func in enumerate((ACT.Sqrt, ACT.Ln, ACT.Tanh, ACT.Sqrt, ACT.Ln)):
                lift_small(BLOCKS - 1, k + 1, func)
            act.wait_ge(adj_used, BLOCKS * CHUNKS)
            for c in split_chunks(HYPER):
                act.wait_ge(nodes_ready, c + 1)
                tiles = slice(c * QT, (c + 1) * QT)
                nc.scalar.activation(hyper_hi[:, tiles, :], lifted[:, tiles, :],
                                     ACT.Copy).then_inc(value_hi_ready, 1)
            act.wait_ge(nodes_ready, BLOCKS)
            round_hi(HYPER, 1, lambda c: hyper(1, c))
            with act.Fori(2, BLOCKS) as b:
                round_hi(HYPER, b, lambda c: hyper(b, c))
            for b in (BLOCKS, BLOCKS + 1):
                for c in range(CHUNKS):
                    hyper(b, c)
            for h in range(2):
                exponentials(0, 0, h)
            attn(0)
            with act.Fori(1, BLOCKS - 1) as b:
                attn(b)
            attn(BLOCKS - 1, last=True)
            act.wait_ge(adj_used, MLP0 * BLOCKS * CHUNKS)
            for r in range(ROUNDS):
                p = MLP0 + r
                if r == 0:
                    round_hi(p, 0, lambda c: small(small_before(ATTN, BLOCKS - 1) + 1, ACT.Sqrt)
                             if c == TAIL_SQRT else None)
                else:
                    round_hi(p, 0, stages(r - 1, BLOCKS - 1))
                if r < ROUNDS - 1:
                    with act.Fori(1, BLOCKS) as b:
                        round_hi(p, b, stages(r, b - 1))
                else:
                    round_hi(p, 1, stages(r, 0))
                    with act.Fori(2, BLOCKS) as b:
                        round_hi(p, b, stages(r, b - 1))
            for stage in range(4):
                mlp(ROUNDS - 1, BLOCKS - 1, stage)

        @block.vector
        def _(dve):
            v = nc.vector
            steps = Steps(dve, dve_steps)
            then = steps.then
            row = [sc[:, k, :] for k in range(24)]
            A, B, C, R, Q = row[:5]
            HALF = slice(0, QT)
            REST = slice(QT, 2 * QT)

            def at(buffer, b):
                return buffer[:, bass.ds(b * QT, QT), :]

            def tiles(x):
                return x[:, :].rearrange("p (q f) -> p q f", q=QT)

            def per_row(x):
                return x.unsqueeze(2).to_broadcast([P, QT, F])

            def per_feature(k):
                return brow[:, k, :].unsqueeze(1).to_broadcast([P, QT, F])

            def tt(o, a, b, op):
                return v.tensor_tensor(o, a, b, op)

            def ts(o, a, s1, s2, op0, op1=None):
                return v.tensor_scalar(o, a, s1, s2, op0, *([op1] if op1 is not None else []))

            def stt(o, a, s, b, op0, op1):
                return v.scalar_tensor_tensor(o, a, s, b, op0, op1)

            def layernorm_ask(y, part=HALF):
                for q in range(QT):
                    last = v.bn_stats(stats[:, q, :], y[:, q, :])
                then(last)
                for q in range(QT):
                    last = v.bn_aggr(mv[:, q, :], stats[:, q, :])
                then(last)
                ts(s_in[:, part], mv[:, :, 1], LN_EPS, None, ALU.add).then_inc(small_asked, 1)

            def layernorm_end(y, o, n, done, part=HALF):
                dve.wait_ge(small_done, n)
                then(v.reciprocal(row[5], s_out[:, part]))
                for q in range(QT):
                    last = ts(o[:, q, :], y[:, q, :], mv[:, q, 0:1], row[5][:, q:q + 1],
                              ALU.subtract, ALU.mult)
                done(last)

            def layernorm(y, o, n, done):
                layernorm_ask(y)
                layernorm_end(y, o, n, done)

            def atanh_ask(norm):
                c, u, small, sq = row[6], row[7], row[9], row[10]
                then(ts(c, norm, MAX_TANH, None, ALU.min))
                ts(u, c, -1.0, 1.0, ALU.mult, ALU.add)
                then(tt(sq, c, c, ALU.mult))
                then(v.reciprocal(u, u))
                stt(s_in[:, HALF], c, 1.0, u, ALU.add, ALU.mult).then_inc(small_asked, 1)
                then(ts(small, sq, 1 / 9, 1 / 7, ALU.mult, ALU.add))
                for term in (1 / 5, 1 / 3, 1.0):
                    then(tt(small, small, sq, ALU.mult))
                    then(ts(small, small, term, None, ALU.add))
                then(tt(small, small, c, ALU.mult))

            def atanh_end(norm, o, n):
                c, u, lg, small, near = row[6], row[7], row[8], row[9], row[11]
                dve.wait_ge(small_done, n)
                then(ts(lg, s_out[:, HALF], 0.5, None, ALU.mult))
                then(tt(small, small, lg, ALU.subtract))
                then(ts(near, c, 0.125, None, ALU.is_lt))
                then(tt(small, small, near, ALU.mult))
                then(tt(lg, lg, small, ALU.add))
                then(v.reciprocal(u, norm))
                then(tt(o, lg, u, ALU.mult))

            def mobius_ask(root):
                nu = row[12]
                then(tt(nu, C, root, ALU.mult))
                then(ts(nu, nu, EPS, None, ALU.max))
                v.tensor_copy(s_in[:, HALF], nu).then_inc(small_asked, 1)

            def mobius_end(bias, n):
                nu, th, x2, xy, den = row[12:17]
                dve.wait_ge(small_done, n)
                then(v.reciprocal(nu, nu))
                then(tt(th, s_out[:, HALF], C, ALU.mult))
                then(tt(th, th, nu, ALU.mult))
                then(tt(x2, th, th, ALU.mult))
                then(tt(x2, x2, Q, ALU.mult))
                then(stt(xy, th, 2.0, R, ALU.mult, ALU.mult))
                then(ts(xy, xy, 1.0, None, ALU.add))
                then(stt(den, x2, bias_sq[:, bias:bias + 1], xy, ALU.mult, ALU.add))
                then(ts(den, den, EPS, None, ALU.max))
                then(v.reciprocal(den, den))
                then(ts(xy, xy, bias_sq[:, bias:bias + 1], None, ALU.add))
                then(tt(xy, xy, th, ALU.mult))
                then(tt(A, xy, den, ALU.mult))
                then(ts(x2, x2, -1.0, 1.0, ALU.mult, ALU.add))
                then(tt(B, x2, den, ALU.mult))

            def moved(y, o, scratch, bias):
                tt(tiles(o), tiles(y), per_row(A), ALU.mult)
                then(tt(tiles(scratch), per_feature(bias), per_row(B), ALU.mult))
                then(tt(o[:, :], o[:, :], scratch[:, :], ALU.add))

            def subtract_at(b, place):
                for c in GRU_LO_AT[place]:
                    subtract_chunk(GRU, b + 1, c)

            def gru(b, lifting=None, splitting=True):
                def lifting_stage(stage):
                    if lifting is not None:
                        stage(lifting)

                def split_at(place):
                    if splitting:
                        subtract_at(b, place)

                feats = xT[:, bass.ds(b * BW, BW)]
                lifting_stage(lift_norms)
                lifting_stage(lift_log)
                split_at(0)
                lifting_stage(lift_exp)
                split_at(1)
                lifting_stage(lift_factors)
                dve.wait_ge(gate_rz, b + 1)
                then(stt(t[1][:, :], e[4][:, :], cols[:, C_HH + 2:C_HH + 3], t[1][:, :],
                         ALU.add, ALU.mult))
                tt(t[1][:, :], t[1][:, :], e[3][:, :], ALU.add).then_inc(gate_lin, 1)
                dve.wait_ge(gate_new, b + 1)
                then(tt(t[1][:, :], feats, t[3][:, :], ALU.subtract))
                then(tt(t[1][:, :], t[1][:, :], t[2][:, :], ALU.mult))
                then(tt(t[1][:, :], t[1][:, :], t[3][:, :], ALU.add))
                tt(t[3][:, :], feats, t[1][:, :], ALU.add).then_inc(dve_part, 1)
                lifting_stage(lift_sum)
                split_at(2)
                dve.wait_ge(mm_done, mm_before(GRU, b) + 3)
                layernorm_ask(tiles(e[5]), part=REST)
                split_at(3)
                layernorm_end(tiles(e[5]), tiles(t[4]), gru_norm_ask(b),
                              lambda i: i.then_inc(ln_out, 1), part=REST)
                lifting_stage(lift_log_back)
                lifting_stage(lift_end)

            def lift_norms(b):
                y, h, s1, s2 = lift
                dve.wait_ge(w_copied, b + 1)
                tt(tiles(s1), at(x_gru, b), at(x_gru, b), ALU.mult)
                tt(s2, y, y, ALU.mult)
                then(tt(tiles(h), tiles(y), per_feature(R_EMBED), ALU.mult))
                v.tensor_reduce(s_in[:, HALF], tiles(s1), AX.X, ALU.add)
                v.tensor_reduce(R, tiles(h), AX.X, ALU.add)
                then(v.tensor_reduce(Q, tiles(s2), AX.X, ALU.add))
                v.tensor_copy(x_sq[:, bass.ds(b * QT, QT)], s_in[:, HALF])
                v.tensor_copy(s_in[:, REST], Q).then_inc(small_asked, 1)

            def lift_log(b):
                dve.wait_ge(small_done, lift_ask(b, 1))
                norm, root = row[17], row[18]
                ts(norm, s_out[:, HALF], EPS, None, ALU.max)
                then(v.tensor_copy(root, s_out[:, REST]))
                atanh_ask(norm)

            def lift_exp(b):
                atanh_end(row[17], C, lift_ask(b, 2))
                mobius_ask(row[18])

            def lift_factors(b):
                mobius_end(0, lift_ask(b, 3))

            def lift_sum(b):
                y, h, s1, s2 = lift
                moved(y, h, s1, R_EMBED)
                then(tt(s1, h, h, ALU.mult))
                then(v.tensor_reduce(s_in[:, HALF], tiles(s1), AX.X, ALU.add))

            def lift_log_back(b):
                dve.wait_ge(small_done, lift_ask(b, 4))
                then(ts(row[17], s_out[:, HALF], EPS, None, ALU.max))
                atanh_ask(row[17])

            def lift_end(b):
                atanh_end(row[17], C, lift_ask(b, 5))
                tt(at(lifted, b), tiles(lift[1]), per_row(C), ALU.mult).then_inc(nodes_ready, 1)
                dve.wait_ge(nodes_ready, b + 1)

            def hyper_norm(b):
                dve.wait_ge(mm_done, mm_before(HYPER, b) + 1)
                v.tensor_copy(row[17], e[1][:, 0:QT])
                v.tensor_copy(s_in[:, HALF], e[1][:, 0:QT]).then_inc(small_asked, 1)

            def hyper_tanh(b):
                dve.wait_ge(small_done, small_before(HYPER, b) + 1)
                na = row[18]
                then(ts(na, s_out[:, HALF], EPS, None, ALU.max))
                v.tensor_copy(s_in[:, HALF], na).then_inc(small_asked, 1)
                then(v.reciprocal(na, na))

            def hyper_layer(b):
                dve.wait_ge(small_done, small_before(HYPER, b) + 2)
                qa, na, beta = row[17], row[18], row[19]
                then(tt(beta, s_out[:, HALF], na, ALU.mult))
                tt(tiles(t[0]), tiles(e[0]), per_row(beta), ALU.mult)
                then(tt(qa, qa, beta, ALU.mult))
                dve.wait_ge(top_copied, b + 1)
                tt(tiles(t[0]), tiles(t[0]), at(top_part, b), ALU.add)
                then(tt(qa, qa, beta, ALU.mult))
                tt(s_in[:, HALF], qa, x_sq[:, bass.ds(b * QT, QT)], ALU.add)
                tt(t[1][:, :], t[0][:, :], t[0][:, :], ALU.mult)
                then(tt(tiles(t[2]), tiles(t[0]), per_feature(R_LAYER), ALU.mult))
                v.tensor_reduce(R, tiles(t[2]), AX.X, ALU.add)
                then(v.tensor_reduce(Q, tiles(t[1]), AX.X, ALU.add))
                v.tensor_copy(s_in[:, REST], Q).then_inc(small_asked, 1)

            def hyper_log(b):
                dve.wait_ge(small_done, small_before(HYPER, b) + 3)
                na, root = row[18], row[20]
                ts(na, s_out[:, HALF], EPS, None, ALU.max)
                then(v.tensor_copy(root, s_out[:, REST]))
                atanh_ask(na)

            def hyper_exp(b):
                atanh_end(row[18], C, small_before(HYPER, b) + 4)
                mobius_ask(row[20])

            def hyper_sum(b):
                mobius_end(1, small_before(HYPER, b) + 5)
                moved(t[0], t[1], t[2], R_LAYER)
                then(tt(tiles(t[1]), tiles(t[1]), at(x_gru, b), ALU.add))
                layernorm_ask(tiles(t[1]))

            def hyper_end(b):
                layernorm_end(tiles(t[1]), tiles(t[2]), small_before(HYPER, b) + 6, then)
                v.tensor_copy(at(x_hyper, b), tiles(t[2])).then_inc(nodes_ready, 1)
                then(tt(tiles(t[3]), tiles(t[2]), per_feature(R_HV), ALU.mult))
                then(v.tensor_reduce(row[0], tiles(t[3]), AX.X, ALU.add))
                if not isinstance(b, int) or b > 0:
                    dve.wait_ge(score_turned, b)
                v.tensor_copy(tiles(t[4]), per_row(row[0])).then_inc(score_made, 1)

            def hyper(b, c):
                early = {3: hyper_norm, 4: hyper_tanh, 5: hyper_layer, 6: hyper_log, 7: hyper_exp}
                late = {0: hyper_sum, 2: hyper_end}
                if c in late and in_pass(b - 2):
                    late[c](b - 2)
                if c in early and in_pass(b - 1):
                    early[c](b - 1)

            def logits(b, k):
                for h in (1, 0):
                    dve.wait_ge(adj_loaded[2 * k + h], b * 16 + (ATTN * BLOCKS + 1) * 16)
                    half = ring[:, 2 * k + h, :, :].rearrange("p q w -> p (q w)")
                    got = ts(mask[:, h, :], half, 0.0, NEG, ALU.is_equal, ALU.mult)
                    if h:
                        got.then_inc(masked, 1)
                    else:
                        then(got)
                        then(tt(half, half, score_row[:, 0:HALF_ROW], ALU.mult))
                for h in range(2):
                    half = ring[:, 2 * k + h, :, :].rearrange("p q w -> p (q w)")
                    then(v.tensor_tensor_reduce(
                        out=half, in0=half, in1=mask[:, h, :], scale=1.0, scalar=LOWEST,
                        op0=ALU.add, op1=ALU.max, accum_out=half_max[:, h:h + 1]))
                    if h == 0:
                        dve.wait_ge(scaled, b * QT + (k + 1))
                        then(ts(absorbed[:, :], half_max[:, 0:1], 1.0, None, ALU.mult))
                ts(minus_max[:, b % 2, k:k + 1], half_max[:, 1:2], half_max[:, 0:1], -1.0,
                   ALU.max, ALU.mult).then_inc(logits_ready, 1)

            def split_value(r, b, x):
                hi, lo = split[r % 2]
                then(v.tensor_copy(at(hi, b), tiles(x)))
                tt(at(lo, b), tiles(x), at(hi, b).bitcast(FP32),
                   ALU.subtract).then_inc(nodes_ready, 1)

            def attn_norm(b):
                if not isinstance(b, int) or b > 0:
                    dve.wait_ge(norm_ready, b)
                dve.wait_ge(adj_used, b * CHUNKS + (ATTN * BLOCKS + 1) * CHUNKS)
                total, neighbours = row[17], row[18]
                then(tt(total, half_sum[:, b % 2, 0, :], half_sum[:, b % 2, 1, :], ALU.add))
                ts(neighbours, minus_max[:, b % 2, :], -NEG, None, ALU.is_lt)
                then(v.reciprocal(total, total))
                then(tt(total, total, neighbours, ALU.mult))
                then(tt(tiles(t[3]), tiles(acc[:, b % 2, :]), per_row(total), ALU.mult))
                tt(tiles(t[3]), tiles(t[3]), at(x_hyper, b), ALU.add).then_inc(agg_copied, 1)
                dve.wait_ge(agg_copied, b + (ATTN * BLOCKS + 1))
                layernorm_ask(tiles(t[3]))

            def attn_norm_end(b):
                layernorm_end(tiles(t[3]), at(x_attn, b), small_before(ATTN, b) + 1,
                              lambda i: i.then_inc(norm_ready, 1))

            def attn(b, before=None):
                for k in range(QT):
                    logits(b, k)
                    if before is not None and k == ATTN_ASK:
                        attn_norm(before)
                    if before is not None and k == ATTN_END:
                        attn_norm_end(before)

            def leaky(o, x):
                return stt(o, x, SLOPE, x, ALU.mult, ALU.max)

            def mlp(r, b, stage):
                p = MLP0 + r
                if stage < 2:
                    dve.wait_ge(hidden_lin, 2 * b + (2 * r * BLOCKS + stage + 1))
                    leaky(t[stage][:, :], t[2 + stage][:, :]).then_inc(dve_part, 1)
                    return
                dve.wait_ge(mm_done, mm_before(p, b) + 3)
                then(tt(tiles(t[4]), tiles(e[2]), per_feature((R_UV, R_VU)[r % 2]), ALU.add))
                then(leaky(t[5][:, :], t[4][:, :]))
                if p < PASSES - 1:
                    split_value(r + 1, b, t[5])
                else:
                    then(tt(tiles(t[5]), tiles(t[5]), at(x_attn, b), ALU.add))
                    layernorm(tiles(t[5]), at(result, b), small_before(p, b) + 1,
                              lambda i: i.then_inc(out_ready, 1))

            def subtract_chunk(p, b, c):
                for h in range(2):
                    n = 2 * c + h
                    if n in pool_halves(p):
                        continue
                    part = slice(h * HALF_QT, (h + 1) * HALF_QT)
                    dve.wait_ge(hi_ready, split_count(p, b, n))
                    tt(adj_lo[:, c, part, :], ring[:, c, part, :],
                       adj_hi[hi_buffer(p, c, h)][:, :, :].bitcast(FP32),
                       ALU.subtract).then_inc(lo_ready, 1)

            def subtract_hi(p, b, after):
                for c in range(CHUNKS):
                    if not whole(p, c):
                        subtract_chunk(p, b, c)
                    after(c)

            def stages(r, b):
                return lambda c: mlp(r, b, DVE_STAGES[c]) if c in DVE_STAGES else None

            dve.wait_ge(params_loaded, 48)
            v.tensor_tensor(bias_rz[:, :], cols[:, C_IH:C_IH + 2], cols[:, C_HH:C_HH + 2], ALU.add)
            v.memset(s_in[:, :], 1.0)
            for k, r in enumerate((R_EMBED, R_LAYER)):
                then(tt(t[k][:, 0:F], brow[:, r, :], brow[:, r, :], ALU.mult))
                last = v.tensor_reduce(bias_sq[:, k:k + 1], t[k][:, 0:F], AX.X, ALU.add)
            last.then_inc(bias_ready, 1)
            dve.wait_ge(bias_ready, 1)
            dve.wait_ge(feats_loaded, 16)
            steps.restart()
            for m, c in enumerate(split_chunks(GRU)):
                dve.wait_ge(adj_used, c + 1)
                dve.wait_ge(x_hi_ready, m + 1)
                tt(at(x_lo, c), at(x_in, c), x_hi[:, m, :, :].bitcast(FP32),
                   ALU.subtract).then_inc(x_lo_ready, 1)
            gru(0)
            with dve.Fori(1, BLOCKS - 1) as b:
                steps.restart()
                gru(b, b - 1)
            steps.restart()
            gru(BLOCKS - 1, BLOCKS - 2, splitting=False)
            steps.restart()
            for stage in (lift_norms, lift_log, lift_exp, lift_factors, lift_sum):
                stage(BLOCKS - 1)
            v.memset(s_in[:, REST], 1.0).then_inc(small_asked, 1)
            lift_log_back(BLOCKS - 1)
            lift_end(BLOCKS - 1)
            for m, c in enumerate(split_chunks(HYPER)):
                dve.wait_ge(adj_used, BLOCKS * CHUNKS + (c + 1))
                dve.wait_ge(value_hi_ready, m + 1)
                tt(at(hyper_lo, c), at(lifted, c), at(hyper_hi, c).bitcast(FP32),
                   ALU.subtract).then_inc(value_lo_ready, 1)
            steps.restart()
            subtract_hi(HYPER, 1, lambda c: hyper(1, c))
            with dve.Fori(2, BLOCKS) as b:
                steps.restart()
                subtract_hi(HYPER, b, lambda c: hyper(b, c))
            steps.restart()
            for b in (BLOCKS, BLOCKS + 1):
                for c in range(CHUNKS):
                    hyper(b, c)
            dve.wait_ge(score_ready, BLOCKS)
            steps.restart()
            attn(0)
            with dve.Fori(1, BLOCKS) as b:
                steps.restart()
                attn(b, b - 1)
            for r in range(ROUNDS):
                steps.restart()
                p = MLP0 + r
                if r == 0:
                    def tail(c):
                        if c == TAIL_ASK:
                            attn_norm(BLOCKS - 1)
                        if c == TAIL_END:
                            attn_norm_end(BLOCKS - 1)

                    subtract_hi(p, 0, tail)
                else:
                    subtract_hi(p, 0, stages(r - 1, BLOCKS - 1))
                with dve.Fori(1, BLOCKS) as b:
                    steps.restart()
                    subtract_hi(p, b, stages(r, b - 1))
            steps.restart()
            for stage in range(3):
                mlp(ROUNDS - 1, BLOCKS - 1, stage)


def kernel(x, adj, L0_gnn_W_msg, L0_gnn_b_msg, L0_gnn_W_ih, L0_gnn_W_hh, L0_gnn_b_ih, L0_gnn_b_hh,
           L1_gnn_embed, L1_gnn_layer, L1_gnn_embed_bias, L1_gnn_layer_bias, L2_gnn_H_v,
           L3_gnn_v_node_feats, L3_gnn_uv_W1, L3_gnn_uv_b1, L3_gnn_uv_W2, L3_gnn_uv_b2,
           L3_gnn_uv_W3, L3_gnn_uv_b3, L3_gnn_vu_W1, L3_gnn_vu_b1, L3_gnn_vu_W2, L3_gnn_vu_b2,
           L3_gnn_vu_W3, L3_gnn_vu_b3):
    import numpy as np
    import concourse.bacc as bacc
    from concourse.bass_utils import run_bass_kernel_spmd

    def a(v):
        return np.asarray(v)

    adj_blocks = a(adj).reshape(BLOCKS, BW, CHUNKS, QT, P).transpose(0, 2, 4, 3, 1)
    adj_rows = a(adj).reshape(BLOCKS, QT, P, 2, HALF_ROW)
    xs = a(x)
    weights = np.concatenate(
        [a(L0_gnn_W_msg).T, a(L0_gnn_W_ih).T, a(L0_gnn_W_hh).T, a(L1_gnn_embed),
         a(L1_gnn_layer)[:F], a(L1_gnn_layer)[F:], a(L3_gnn_uv_W1), a(L3_gnn_uv_W2),
         a(L3_gnn_uv_W3), a(L3_gnn_vu_W1), a(L3_gnn_vu_W2), a(L3_gnn_vu_W3)], axis=1)
    columns = np.stack(
        [a(L0_gnn_b_msg), *a(L0_gnn_b_ih).reshape(3, F), *a(L0_gnn_b_hh).reshape(3, F),
         a(L3_gnn_uv_b1), a(L3_gnn_uv_b2), a(L3_gnn_vu_b1), a(L3_gnn_vu_b2)], axis=1)
    rows = np.concatenate([a(L1_gnn_embed_bias), a(L1_gnn_layer_bias), a(L2_gnn_H_v)[:, 0],
                           a(L3_gnn_uv_b3), a(L3_gnn_vu_b3)])[None, :]
    arrays = {
        "adj": adj_blocks, "adj_rows": adj_rows, "x_nodes": xs.reshape(TILES, P, F).transpose(1, 0, 2),
        "x_feats": xs.T, "weights": weights.reshape(F, W_ALL, P), "columns": columns, "rows": rows,
    }
    arrays = {f"in_{k}": np.ascontiguousarray(v) for k, v in arrays.items()}
    nc = bacc.Bacc("TRN2", target_bir_lowering=False, num_devices=1)
    args = [nc.dram_tensor(k, v.shape, FP32, kind="ExternalInput").ap() for k, v in arrays.items()]
    args.append(nc.dram_tensor("out", (P, TILES, F), FP32, kind="ExternalOutput").ap())
    build(nc, *args)
    r = run_bass_kernel_spmd(nc, [arrays], core_ids=[0])
    return np.ascontiguousarray(np.asarray(r.results[0]["out"]).transpose(1, 0, 2)).reshape(N, F)
```
